# Optimizing a Trainium2 kernel written in Bass

```python
import numpy as np
import jax
import jax.numpy as jnp

def _softmax(x, axis=-1):
    return jax.nn.softmax(x, axis=axis)

def _gelu(x):
    return jax.nn.gelu(x, approximate=True)

def _silu(x):
    return jax.nn.silu(x)

def _sigmoid(x):
    return jax.nn.sigmoid(x)

def _layernorm(x, axis=-1, eps=1e-05):
    m = jnp.mean(x, axis=axis, keepdims=True)
    v = jnp.var(x, axis=axis, keepdims=True)
    return (x - m) / jnp.sqrt(v + eps)

def _scatter_add(tgt, idx, src, axis=0):
    return tgt.at[idx].add(src)

def _segment_sum(src, seg, n):
    return jax.ops.segment_sum(src, seg, n)
kernel_name = 'mk_macaron_d1_jaxref_r8_a635c9'

def setup_inputs(seed: int=0):
    np.random.seed(seed)
    _w = jnp.asarray

    def _L0_attn_setup():
        import jax, jax.numpy as jnp
        import numpy as np
        import math
        NUM_HEADS = 16

        def get_slopes(n):

            def pow2(n):
                start = 2 ** (-2 ** (-(math.log2(n) - 3)))
                return [start * start ** i for i in range(n)]
            if math.log2(n).is_integer():
                return pow2(n)
            c = 2 ** math.floor(math.log2(n))
            return pow2(c) + get_slopes(2 * c)[0::2][:n - c]
        key = jax.random.key(seed)
        ks = jax.random.split(key, 5)
        B, T, C = (2, 256, 128)
        return {'x': jax.random.normal(ks[0], (B, T, C), dtype=jnp.float32), 'W_qkv': jax.random.normal(ks[1], (C, 3 * C), dtype=jnp.float32) * 0.02, 'b_qkv': jax.random.normal(ks[2], (3 * C,), dtype=jnp.float32) * 0.02, 'W_proj': jax.random.normal(ks[3], (C, C), dtype=jnp.float32) * 0.02, 'b_proj': jax.random.normal(ks[4], (C,), dtype=jnp.float32) * 0.02}
    _L0_attn_in = _L0_attn_setup()

    def _L0_ffn_setup():
        import jax, jax.numpy as jnp
        import numpy as np
        DIM = 128
        DEPTH = 6
        HEADS = 16
        DIM_HEAD = 64
        WINDOW = 32
        INNER = HEADS * DIM_HEAD
        DIM_INNER = int(DIM * 4 * 2 / 3)
        QK_SCALE = 8.0

        def shift_tokens(t):
            a, s = jnp.split(t, 2, -1)
            s = jnp.pad(s, ((0, 0), (1, 0), (0, 0)))[:, :-1]
            return jnp.concatenate([a, s], -1)

        def l2norm(t):
            return t / jnp.maximum(jnp.linalg.norm(t, axis=-1, keepdims=True), 1e-12)

        def rotate_half(x):
            x1, x2 = jnp.split(x, 2, -1)
            return jnp.concatenate([-x2, x1], -1)

        def rotary_tables(n):
            half = jnp.arange(0, DIM_HEAD, 2, dtype=jnp.float32)
            inv_freq = 1.0 / 10000.0 ** (half / DIM_HEAD)
            t = jnp.arange(n, dtype=jnp.float32)
            freqs = t[:, None] * inv_freq[None, :]
            freqs = jnp.concatenate([freqs, freqs], -1)
            base_scale = (half + 0.4 * DIM_HEAD) / (1.4 * DIM_HEAD)
            power = (t - n // 2) / (WINDOW // 2)
            scale = base_scale[None, :] ** power[:, None]
            scale = jnp.concatenate([scale, scale], -1)
            return (freqs, scale)

        def local_attention(q, k, v):
            b, h, n, d = q.shape
            w = WINDOW
            nw = n // w
            bq = q.reshape(b, h, nw, w, d)
            bk = k.reshape(b, h, nw, w, d)
            bv = v.reshape(b, h, nw, w, d)

            def look(t):
                p = jnp.pad(t, ((0, 0), (0, 0), (1, 0), (0, 0), (0, 0)))
                return jnp.concatenate([p[:, :, :nw], p[:, :, 1:]], axis=3)
            bk2, bv2 = (look(bk), look(bv))
            seq = jnp.arange(n).reshape(nw, w)
            seq_p = jnp.pad(seq, ((1, 0), (0, 0)), constant_values=-1)
            jt = jnp.concatenate([seq_p[:nw], seq_p[1:]], axis=1)
            it = seq[:, :, None]
            jb = jt[:, None, :]
            mask = (it < jb) | (it > jb + w) | (jb == -1)
            sim = jnp.einsum('bhwie,bhwje->bhwij', bq, bk2) * QK_SCALE
            sim = jnp.where(mask, -jnp.finfo(sim.dtype).max, sim)
            attn = jax.nn.softmax(sim, -1)
            out = jnp.einsum('bhwij,bhwje->bhwie', attn, bv2)
            return out.reshape(b, h, n, d)

        def attn_layer(x, Wqkv, qs, ksc, Wo):
            b, n, _ = x.shape
            qkv = x @ Wqkv
            q, k, v = jnp.split(qkv, 3, -1)
            sh = lambda t: t.reshape(b, n, HEADS, DIM_HEAD).transpose(0, 2, 1, 3)
            q, k, v = (sh(q), sh(k), sh(v))
            q = l2norm(q) * qs
            k = l2norm(k) * ksc
            freqs, scale = rotary_tables(n)
            cos, sin = (jnp.cos(freqs), jnp.sin(freqs))
            q = q * cos * scale + rotate_half(q) * sin * scale
            inv = 1.0 / scale
            k = k * cos * inv + rotate_half(k) * sin * inv
            out = local_attention(q, k, v)
            out = out.transpose(0, 2, 1, 3).reshape(b, n, INNER)
            return out @ Wo

        def ffn_layer(x, g, bln, W1, b1, W2, b2):
            mu = x.mean(-1, keepdims=True)
            var = ((x - mu) ** 2).mean(-1, keepdims=True)
            xn = (x - mu) / jnp.sqrt(var + 1e-05) * g + bln
            hg = xn @ W1 + b1
            a, gate = jnp.split(hg, 2, -1)
            return a * jax.nn.gelu(gate, approximate=False) @ W2 + b2
        key = jax.random.key(seed)
        ks = jax.random.split(key, 8)
        B, N = (2, 256)
        init = lambda k, shape: jax.random.normal(k, shape, jnp.float32) * 0.02
        return {'x': jax.random.normal(ks[0], (B, N, DIM), jnp.float32), 'Wqkv': init(ks[1], (DEPTH, DIM, 3 * INNER)), 'q_scale': jnp.ones((DEPTH, DIM_HEAD), jnp.float32), 'k_scale': jnp.ones((DEPTH, DIM_HEAD), jnp.float32), 'Wo': init(ks[2], (DEPTH, INNER, DIM)), 'ln_g': jnp.ones((DEPTH, DIM), jnp.float32), 'ln_b': jnp.zeros((DEPTH, DIM), jnp.float32), 'W1': init(ks[3], (DEPTH, DIM, 2 * DIM_INNER)), 'b1': jnp.zeros((DEPTH, 2 * DIM_INNER), jnp.float32), 'W2': init(ks[4], (DEPTH, DIM_INNER, DIM)), 'b2': jnp.zeros((DEPTH, DIM), jnp.float32)}
    _L0_ffn_in = _L0_ffn_setup()
    _d = {'L0_attn_x': _L0_attn_in['x'], 'L0_attn_W_qkv': _L0_attn_in['W_qkv'], 'L0_attn_b_qkv': _L0_attn_in['b_qkv'], 'L0_attn_W_proj': _L0_attn_in['W_proj'], 'L0_attn_b_proj': _L0_attn_in['b_proj'], 'L0_ffn_Wqkv': _L0_ffn_in['Wqkv'], 'L0_ffn_q_scale': _L0_ffn_in['q_scale'], 'L0_ffn_k_scale': _L0_ffn_in['k_scale'], 'L0_ffn_Wo': _L0_ffn_in['Wo'], 'L0_ffn_ln_g': _L0_ffn_in['ln_g'], 'L0_ffn_ln_b': _L0_ffn_in['ln_b'], 'L0_ffn_W1': _L0_ffn_in['W1'], 'L0_ffn_b1': _L0_ffn_in['b1'], 'L0_ffn_W2': _L0_ffn_in['W2'], 'L0_ffn_b2': _L0_ffn_in['b2']}
    _x0 = _d['L0_attn_x']
    _d['L0_attn_x'] = jax.random.normal(jax.random.fold_in(jax.random.key(seed), 1), (4, 512, 128), dtype=_x0.dtype)
    del _x0
    return _d

def reference(L0_attn_x, L0_attn_W_qkv, L0_attn_b_qkv, L0_attn_W_proj, L0_attn_b_proj, L0_ffn_Wqkv, L0_ffn_q_scale, L0_ffn_k_scale, L0_ffn_Wo, L0_ffn_ln_g, L0_ffn_ln_b, L0_ffn_W1, L0_ffn_b1, L0_ffn_W2, L0_ffn_b2):

    def _L0_attn_ref(x, W_qkv, b_qkv, W_proj, b_proj):
        import jax, jax.numpy as jnp
        import numpy as np
        import math
        NUM_HEADS = 16

        def get_slopes(n):

            def pow2(n):
                start = 2 ** (-2 ** (-(math.log2(n) - 3)))
                return [start * start ** i for i in range(n)]
            if math.log2(n).is_integer():
                return pow2(n)
            c = 2 ** math.floor(math.log2(n))
            return pow2(c) + get_slopes(2 * c)[0::2][:n - c]
        B, T, C = x.shape
        H = NUM_HEADS
        D = C // H
        qkv = x @ W_qkv + b_qkv
        q, k, v = jnp.split(qkv, 3, axis=-1)
        q = q.reshape(B, T, H, D).transpose(0, 2, 1, 3)
        k = k.reshape(B, T, H, D).transpose(0, 2, 1, 3)
        v = v.reshape(B, T, H, D).transpose(0, 2, 1, 3)
        slopes = jnp.asarray(get_slopes(H), dtype=jnp.float32)
        idx = jnp.arange(T)
        alibi = jnp.minimum(idx[None, :] - idx[:, None], 0).astype(jnp.float32)
        bias = slopes[:, None, None] * alibi
        scale = 1.0 / math.sqrt(D)
        scores = jnp.einsum('bhtd,bhsd->bhts', q, k) * scale + bias[None]
        w = jax.nn.softmax(scores, axis=-1)
        y = jnp.einsum('bhts,bhsd->bhtd', w, v)
        y = y.transpose(0, 2, 1, 3).reshape(B, T, C)
        return y @ W_proj + b_proj

    def _L0_ffn_ref(x, Wqkv, q_scale, k_scale, Wo, ln_g, ln_b, W1, b1, W2, b2):
        import jax, jax.numpy as jnp
        import numpy as np
        DIM = 128
        DEPTH = 6
        HEADS = 16
        DIM_HEAD = 64
        WINDOW = 32
        INNER = HEADS * DIM_HEAD
        DIM_INNER = int(DIM * 4 * 2 / 3)
        QK_SCALE = 8.0

        def shift_tokens(t):
            a, s = jnp.split(t, 2, -1)
            s = jnp.pad(s, ((0, 0), (1, 0), (0, 0)))[:, :-1]
            return jnp.concatenate([a, s], -1)

        def l2norm(t):
            return t / jnp.maximum(jnp.linalg.norm(t, axis=-1, keepdims=True), 1e-12)

        def rotate_half(x):
            x1, x2 = jnp.split(x, 2, -1)
            return jnp.concatenate([-x2, x1], -1)

        def rotary_tables(n):
            half = jnp.arange(0, DIM_HEAD, 2, dtype=jnp.float32)
            inv_freq = 1.0 / 10000.0 ** (half / DIM_HEAD)
            t = jnp.arange(n, dtype=jnp.float32)
            freqs = t[:, None] * inv_freq[None, :]
            freqs = jnp.concatenate([freqs, freqs], -1)
            base_scale = (half + 0.4 * DIM_HEAD) / (1.4 * DIM_HEAD)
            power = (t - n // 2) / (WINDOW // 2)
            scale = base_scale[None, :] ** power[:, None]
            scale = jnp.concatenate([scale, scale], -1)
            return (freqs, scale)

        def local_attention(q, k, v):
            b, h, n, d = q.shape
            w = WINDOW
            nw = n // w
            bq = q.reshape(b, h, nw, w, d)
            bk = k.reshape(b, h, nw, w, d)
            bv = v.reshape(b, h, nw, w, d)

            def look(t):
                p = jnp.pad(t, ((0, 0), (0, 0), (1, 0), (0, 0), (0, 0)))
                return jnp.concatenate([p[:, :, :nw], p[:, :, 1:]], axis=3)
            bk2, bv2 = (look(bk), look(bv))
            seq = jnp.arange(n).reshape(nw, w)
            seq_p = jnp.pad(seq, ((1, 0), (0, 0)), constant_values=-1)
            jt = jnp.concatenate([seq_p[:nw], seq_p[1:]], axis=1)
            it = seq[:, :, None]
            jb = jt[:, None, :]
            mask = (it < jb) | (it > jb + w) | (jb == -1)
            sim = jnp.einsum('bhwie,bhwje->bhwij', bq, bk2) * QK_SCALE
            sim = jnp.where(mask, -jnp.finfo(sim.dtype).max, sim)
            attn = jax.nn.softmax(sim, -1)
            out = jnp.einsum('bhwij,bhwje->bhwie', attn, bv2)
            return out.reshape(b, h, n, d)

        def attn_layer(x, Wqkv, qs, ksc, Wo):
            b, n, _ = x.shape
            qkv = x @ Wqkv
            q, k, v = jnp.split(qkv, 3, -1)
            sh = lambda t: t.reshape(b, n, HEADS, DIM_HEAD).transpose(0, 2, 1, 3)
            q, k, v = (sh(q), sh(k), sh(v))
            q = l2norm(q) * qs
            k = l2norm(k) * ksc
            freqs, scale = rotary_tables(n)
            cos, sin = (jnp.cos(freqs), jnp.sin(freqs))
            q = q * cos * scale + rotate_half(q) * sin * scale
            inv = 1.0 / scale
            k = k * cos * inv + rotate_half(k) * sin * inv
            out = local_attention(q, k, v)
            out = out.transpose(0, 2, 1, 3).reshape(b, n, INNER)
            return out @ Wo

        def ffn_layer(x, g, bln, W1, b1, W2, b2):
            mu = x.mean(-1, keepdims=True)
            var = ((x - mu) ** 2).mean(-1, keepdims=True)
            xn = (x - mu) / jnp.sqrt(var + 1e-05) * g + bln
            hg = xn @ W1 + b1
            a, gate = jnp.split(hg, 2, -1)
            return a * jax.nn.gelu(gate, approximate=False) @ W2 + b2
        for i in range(DEPTH):
            x = attn_layer(shift_tokens(x), Wqkv[i], q_scale[i], k_scale[i], Wo[i]) + x
            x = ffn_layer(shift_tokens(x), ln_g[i], ln_b[i], W1[i], b1[i], W2[i], b2[i]) + x
        return x
    x = L0_attn_x
    x = x + 0.5 * _L0_ffn_ref(_layernorm(x, axis=-1), L0_ffn_Wqkv, L0_ffn_q_scale, L0_ffn_k_scale, L0_ffn_Wo, L0_ffn_ln_g, L0_ffn_ln_b, L0_ffn_W1, L0_ffn_b1, L0_ffn_W2, L0_ffn_b2)
    x = x + _L0_attn_ref(_layernorm(x, axis=-1), L0_attn_W_qkv, L0_attn_b_qkv, L0_attn_W_proj, L0_attn_b_proj)
    x = x + 0.5 * _L0_ffn_ref(_layernorm(x, axis=-1), L0_ffn_Wqkv, L0_ffn_q_scale, L0_ffn_k_scale, L0_ffn_Wo, L0_ffn_ln_g, L0_ffn_ln_b, L0_ffn_W1, L0_ffn_b1, L0_ffn_W2, L0_ffn_b2)
    return x

_drawn_inputs = setup_inputs


def setup_inputs(seed=0):
    import zlib

    import numpy as np

    out = dict(_drawn_inputs(seed))
    spreads = {'L0_ffn_q_scale': (1.0, 0.6),
     'L0_ffn_k_scale': (1.0, 0.6),
     'L0_ffn_ln_g': (1.0, 0.6),
     'L0_ffn_ln_b': (0.0, 0.8),
     'L0_ffn_b1': (0.0, 0.8),
     'L0_ffn_b2': (0.0, 0.1)}
    factors = {'L0_attn_W_qkv': 8.0,
     'L0_attn_b_qkv': 8.0,
     'L0_attn_W_proj': 8.0,
     'L0_attn_b_proj': 4.164,
     'L0_ffn_W1': 3.135,
     'L0_ffn_W2': 3.077}
    for name, (base, spread) in spreads.items():
        noise = np.random.default_rng([zlib.crc32(name.encode()), seed]).standard_normal(out[name].shape)
        drawn = base * np.exp(spread * noise) if base else spread * noise
        out[name] = jnp.asarray(drawn.astype(out[name].dtype))
    for name, factor in factors.items():
        out[name] = (out[name] * factor).astype(out[name].dtype)
    return out
```

```python
from contextlib import ExitStack, contextmanager

import numpy as np
import concourse.bass as bass
from concourse import mybir

F32 = mybir.dt.float32
BF16 = mybir.dt.bfloat16
ALU = mybir.AluOpType
ACT = mybir.ActivationFunctionType
AX = mybir.AxisListType.X

P = 128
NB, NT, C = 4, 512, 128
TPS = NT // P
TILES = NB * TPS
DEPTH, HEADS, DH, WIN = 6, 16, 64, 32
INNER = HEADS * DH
PAIRS = HEADS // 2
KEYS = P + WIN
CH = 512
DI = C * 4 * 2 // 3
FCH = [(0, 128), (128, 128), (256, DI - 256)]
QK_SCALE = 8.0
EPS = 1e-5
MASKED = -1e30
H2, D2 = 16, 8
STEPS = DEPTH * NB
CREDIT = 1


def rotary_constants():
    f = np.float32
    half = np.arange(0, DH, 2, dtype=f)
    inv_freq = (f(1.0) / np.power(f(10000.0), half / f(DH))).astype(f)
    t = np.arange(NT, dtype=f)
    freqs = t[:, None] * inv_freq[None, :]
    freqs = np.concatenate([freqs, freqs], -1)
    base = (half + f(0.4 * DH)) / f(1.4 * DH)
    power = (t - f(NT // 2)) / f(WIN // 2)
    scale = np.power(base[None, :], power[:, None]).astype(f)
    scale = np.concatenate([scale, scale], -1)
    cos, sin = np.cos(freqs).astype(f), np.sin(freqs).astype(f)
    sin[:, :DH // 2] *= f(-1.0)
    inv = (f(1.0) / scale).astype(f)
    tabs = np.stack([cos * scale, sin * scale, cos * inv, sin * inv], 1)
    return np.ascontiguousarray(tabs.reshape(TPS, P, 4, DH).transpose(1, 0, 2, 3)).astype(f)


def window_mask():
    d = np.arange(KEYS)[None, :] - np.arange(P)[:, None]
    m = np.where((d >= 0) & (d <= WIN), 0.0, MASKED)
    return np.stack([m, m], 1)


def alibi_slopes():
    start = 2 ** (-2 ** (-(np.log2(H2) - 3)))
    return [float(start * start ** i) for i in range(H2)]


def shift_matrices():
    down, carry = np.eye(P, k=1, dtype=np.float32), np.zeros((P, P), np.float32)
    carry[P - 1, 0] = 1.0
    return np.concatenate([np.eye(P, dtype=np.float32), down, carry], 1)


@contextmanager
def phase_semaphores(nc, tag):
    made = []

    def sem(name):
        made.append(nc.alloc_semaphore(f"{tag}_{name}"))
        return made[-1]

    yield sem
    nc.clear_and_free_semaphores(made)
    nc.all_engine_barrier()


def tile_front(t):
    return [("in", t, 0), ("qkv", t, 0), ("qkv", t, 1), ("nq", t, 0), ("qkv", t, 2), ("qkv", t, 3), ("nk", t, 0),
            ("rot", t, 0), ("rot", t, 1), ("qkv", t, 4), ("rot", t, 2), ("qkv", t, 5), ("rot", t, 3)]


def tile_back(t):
    return [("s", t, 0), ("s", t, 1), ("s", t, 2), ("s", t, 3), ("pt", t, 0), ("s", t, 4), ("s", t, 5),
            ("pv", t, 0), ("pt", t, 1), ("s", t, 6), ("s", t, 7), ("pv", t, 1), ("pt", t, 2), ("pv", t, 2),
            ("pt", t, 3), ("ot", t, 0), ("pv", t, 3), ("ot", t, 1), ("wo", t, 0)]


def merged(a, b):
    at = [((n + 0.5) / len(a), 0, x) for n, x in enumerate(a)] + [((n + 0.5) / len(b), 1, x) for n, x in enumerate(b)]
    return [x for _, _, x in sorted(at, key=lambda y: (y[0], y[1]))]


def step_order():
    order = tile_front(0)
    for t in range(TPS - 1):
        order += merged(tile_back(t), tile_front(t + 1))
    return order + tile_back(TPS - 1) + [("ffn", 0, 0)]


def uses(order, per_part):
    before, n = {}, 0
    for part in order:
        before[part] = n
        n += per_part.get(part[0], 0)
    return before, n


def unit_heads(k):
    return [4 * (k // 2) + k % 2, 4 * (k // 2) + k % 2 + 2]


def layer_norm_phase(nc, tag, x, h, x_in, mix, out_dram):
    with ExitStack() as ctx:
        sem = ctx.enter_context(phase_semaphores(nc, tag))
        stats = ctx.enter_context(nc.sbuf_tensor(f"{tag}_stats", [P, TILES, 6], F32))
        mv = ctx.enter_context(nc.sbuf_tensor(f"{tag}_mv", [P, TILES, 2], F32))
        ve = ctx.enter_context(nc.sbuf_tensor(f"{tag}_ve", [P, TILES], F32))
        mh = ctx.enter_context(nc.sbuf_tensor(f"{tag}_mh", [P, TILES], F32))
        rstd = ctx.enter_context(nc.sbuf_tensor(f"{tag}_rstd", [P, TILES], F32))
        x_loaded, x_ready, stats_ready, mv_ready, ve_ready, mh_ready, rstd_ready, h_ready, stored = [
            sem(n) for n in ("x_loaded", "x_ready", "stats_ready", "mv_ready", "ve_ready", "mh_ready",
                             "rstd_ready", "h_ready", "stored")]
        block = ctx.enter_context(nc.Block())

        @block.sync
        def _(sp):
            if x_in is not None:
                for b in range(NB):
                    sp.dma_start(x[:, b * TPS:(b + 1) * TPS, :],
                                 x_in[b].rearrange("(t p) c -> p t c", p=P)).then_inc(x_loaded, 16)
            if out_dram is not None:
                for b in range(NB):
                    sp.wait_ge(x_ready, b + 1)
                    sp.dma_start(out_dram[b].rearrange("(t p) c -> p t c", p=P),
                                 x[:, b * TPS:(b + 1) * TPS, :]).then_inc(stored, 16)
                sp.wait_ge(stored, 16 * NB)

        @block.vector
        def _(dve):
            if out_dram is None:
                nc.vector.memset(mh[:], -0.5).then_inc(mh_ready, 1)
            for b in range(NB):
                sl = slice(b * TPS, (b + 1) * TPS)
                if x_in is not None:
                    dve.wait_ge(x_loaded, 16 * NB)
                if mix is not None:
                    nc.vector.scalar_tensor_tensor(out=x[:, sl, :], in0=h[:, sl, :], scalar=mix, in1=x[:, sl, :],
                                                   op0=ALU.mult, op1=ALU.add).then_inc(x_ready, 1)
            if out_dram is not None:
                return
            if mix is not None:
                dve.wait_ge(x_ready, NB)
            for n in range(TILES):
                nc.vector.bn_stats(stats[:, n, :], x[:, n, :]).then_inc(stats_ready, 1)
            for n in range(TILES):
                dve.wait_ge(stats_ready, n + 1)
                nc.vector.bn_aggr(mv[:, n, :], stats[:, n, :]).then_inc(mv_ready, 1)
            dve.wait_ge(mv_ready, TILES)
            nc.vector.tensor_scalar(ve[:], mv[:, :, 1], EPS, None, ALU.add).then_inc(ve_ready, 1)
            dve.wait_ge(rstd_ready, 1)
            for n in range(TILES):
                nc.vector.tensor_scalar(h[:, n, :], x[:, n, :], mv[:, n, 0:1], rstd[:, n:n + 1],
                                        ALU.subtract, ALU.mult).then_inc(h_ready, 1)

        @block.gpsimd
        def _(pool):
            if out_dram is None:
                pool.wait_ge(mh_ready, 1)
                pool.wait_ge(ve_ready, 1)
                nc.gpsimd.tensor_tensor(rstd[:], ve[:], mh[:], ALU.pow).then_inc(rstd_ready, 1)


def macaron_phase(nc, tag, h, const, w):
    order = step_order()
    t_use, T_PER = uses(order, {"rot": 1, "pt": 1, "ot": 1})
    m_use, M_PER = uses(order, {"in": 1, "wo": 1, "ffn": 3})
    assert T_PER % 2 == 0
    S_PER = TPS * PAIRS // 2 + len(FCH)

    with ExitStack() as ctx:
        def sb(n, shape, dt=F32):
            return ctx.enter_context(nc.sbuf_tensor(f"{tag}_{n}", shape, dt))

        def ps(n):
            return ctx.enter_context(nc.psum_tensor(f"{tag}_{n}", [P, 512], F32))

        sem = ctx.enter_context(phase_semaphores(nc, tag))

        wqkv = sb("wqkv", [P, 2, 3 * INNER])
        wo = sb("wo", [P, PAIRS, C])
        w1 = sb("w1", [P, 2 * DI])
        w2 = sb("w2", [P, len(FCH), C])
        qk_gain = sb("qk_gain", [P, 2, DH])
        tabs = sb("tabs", [P, TPS, 4, DH])
        ln_g, ln_b = sb("ln_g", [P, 1]), sb("ln_b", [P, 1])
        b1 = sb("b1", [P, 2, len(FCH)])
        b2 = sb("b2", [P, C])
        h_in = sb("h_in", [P, TPS, C])
        h_mid = sb("h_mid", [P, TPS, C])
        xs = sb("xs", [P, NT + 1])
        sq = sb("sq", [P, 2, CH])
        qk = sb("qk", [P, 4, CH])
        swap = sb("swap", [P, 2, CH])
        ss = sb("ss", [P, 2, HEADS])
        ssm = sb("ssm", [P, 2, HEADS])
        rn = sb("rn", [P, 2, HEADS])
        rq8, nrq8 = sb("rq8", [P, TPS, HEADS]), sb("nrq8", [P, TPS, HEADS])
        minus_half = sb("minus_half", [P, HEADS])
        qT = sb("qT", [P, TPS, PAIRS, P])
        kT = sb("kT", [P, TPS, PAIRS, KEYS])
        v = sb("v", [P, TPS, HEADS, DH + 1])
        mx, nb = sb("mx", [P, HEADS]), sb("nb", [P, HEADS])
        pr = sb("pr", [P, HEADS, KEYS])
        prT = sb("prT", [P, 2, 4, P])
        ppT = sb("ppT", [P, HEADS, WIN])
        rden = sb("rden", [P, 4])
        on = sb("on", [P, HEADS, DH])
        oT = sb("oT", [P, PAIRS, P])
        hb = sb("hb", [P, TPS, C])
        fstats = sb("fstats", [P, TPS, 2, 6])
        fmv = sb("fmv", [P, TPS, 2])
        fve, frstd = sb("fve", [P, TPS]), sb("frstd", [P, TPS])
        xn = sb("xn", [P, TPS, C])
        xnT = sb("xnT", [P, NT])
        gate = sb("gate", [P, 2, NT])
        uT = sb("uT", [P, len(FCH), NT])

        QKV = [ps("psQ0"), ps("psQ1")]
        T = [ps("psT0"), ps("psT1")]
        S = [ps("psS0"), ps("psS1")]
        O, M = ps("psO"), ps("psM")

        wqkv_loaded, wo_loaded, wf_loaded, gain_loaded = [sem(n) for n in (
            "wqkv_loaded", "wo_loaded", "wf_loaded", "gain_loaded")]
        (ready0, h_ready, hin_ready, hT_ps, xs_ready, qkv_ps, sq_ready, u_ready, w_ready, rot_ready,
         ssm_ready, rn_ready, rq_ready, kn_ready, qk_ps, qkT_ready, v_ready, s_ps, mx_ready, nb_ready,
         exp_ready, pT_ps, pT_ready, ppT_ready, pv_ps, rden_ready, on_ready, oT_ps, oT_ready, wo_ps,
         hmid_ready, tabs_ready, qkv_used) = [sem(n) for n in (
             "ready0", "h_ready", "hin_ready", "hT_ps", "xs_ready", "qkv_ps", "sq_ready", "u_ready", "w_ready",
             "rot_ready", "ssm_ready", "rn_ready", "rq_ready", "kn_ready", "qk_ps", "qkT_ready", "v_ready",
             "s_ps", "mx_ready", "nb_ready", "exp_ready", "pT_ps", "pT_ready", "ppT_ready", "pv_ps",
             "rden_ready", "on_ready", "oT_ps", "oT_ready", "wo_ps", "hmid_ready", "tabs_ready", "qkv_used")]
        ss_ready = [sem(f"ss_ready{b}") for b in range(2)]
        qkv_free = [sem(f"qkv_free{b}") for b in range(2)]
        t_free = [sem(f"t_free{b}") for b in range(2)]
        s_free = [sem(f"s_free{b}") for b in range(2)]
        half_ready = sem("half_ready")
        o_free, m_free = sem("o_free"), sem("m_free")
        (hb_ready, sh_ps, fst_ready, fmv_ready, fve_ready, frstd_ready, xn_ready, xnT_ps, xnT_ready, gate_ps,
         lin_ps, gate_ready, uT_ready, y_ps) = [sem(n) for n in (
             "hb_ready", "sh_ps", "fst_ready", "fmv_ready", "fve_ready", "frstd_ready", "xn_ready", "xnT_ps",
             "xnT_ready", "gate_ps", "lin_ps", "gate_ready", "uT_ready", "y_ps")]
        block = ctx.enter_context(nc.Block())
        ident, down, carry = const["ident"], const["down"], const["carry"]

        def heads8(ap):
            return ap.rearrange("p (h d) -> p h d", d=DH)

        @block.sync
        def _(sp):
            def load_qkv(l, slot):
                sp.dma_start(wqkv[:, slot, :], w["Wqkv"][l]).then_inc(wqkv_loaded, 16)

            def load_gains(l):
                for n, name in enumerate(("q_scale", "k_scale")):
                    sp.dma_start(qk_gain[:, n, :], w[name][l].partition_broadcast(P)).then_inc(gain_loaded, 16)

            def load_wo(l):
                sp.dma_start(wo[:, :, :], w["Wo"][l].rearrange("(k p) c -> p k c", p=P)).then_inc(wo_loaded, 16)

            def load_ffn(l):
                sp.dma_start(w1[:, :], w["W1"][l]).then_inc(wf_loaded, 16)
                for c, (r0, n) in enumerate(FCH):
                    sp.dma_start(w2[0:n, c, :], w["W2"][l, r0:r0 + n, :]).then_inc(wf_loaded, 16)
                for a in range(2):
                    for c, (r0, n) in enumerate(FCH):
                        sp.dma_start(b1[0:n, a, c:c + 1],
                                     w["b1"][l, a * DI + r0:a * DI + r0 + n].unsqueeze(1)).then_inc(wf_loaded, 16)
                sp.dma_start(b2[:, :], w["b2"][l].partition_broadcast(P)).then_inc(wf_loaded, 16)
                sp.dma_start(ln_g[:, :], w["ln_g"][l].unsqueeze(1)).then_inc(wf_loaded, 16)
                sp.dma_start(ln_b[:, :], w["ln_b"][l].unsqueeze(1)).then_inc(wf_loaded, 16)

            load_gains(0)
            load_qkv(0, 0)
            load_wo(0)
            load_ffn(0)
            with sp.Fori(0, DEPTH - 1) as l:
                sp.wait_ge(qkv_ps, 6 * TILES * l + 1)
                load_qkv(l + 1, (l + 1) % 2)
                sp.wait_ge(tabs_ready, l + 1)
                load_gains(l + 1)
                sp.wait_ge(wo_ps, TILES * l + TILES)
                load_wo(l + 1)
                sp.wait_ge(h_ready, NB * l + 2 * NB)
                load_ffn(l + 1)

        N_WF = 16 * (1 + len(FCH) + 2 * len(FCH) + 3)

        @block.gpsimd
        def _(pool):
            nc.gpsimd.memset(minus_half[:], -0.5).then_inc(half_ready, 1)
            pool.wait_ge(half_ready, 1)
            with pool.Fori(0, DEPTH) as l:
                pool.wait_ge(gain_loaded, 32 * l + 32)
                pool.wait_ge(w_ready, CREDIT + 4 * TILES * l)
                for n in range(2):
                    g = qk_gain[:, n, :].unsqueeze(1).broadcast_to([P, TPS, DH])
                    nc.gpsimd.tensor_tensor(tabs[:, :, 2 * n, :], const["rotary"][:, :, 2 * n, :], g, ALU.mult)
                    for a, b in ((0, DH // 2), (DH // 2, 0)):
                        g = qk_gain[:, n, b:b + DH // 2].unsqueeze(1).broadcast_to([P, TPS, DH // 2])
                        last = nc.gpsimd.tensor_tensor(tabs[:, :, 2 * n + 1, a:a + DH // 2],
                                                       const["rotary"][:, :, 2 * n + 1, a:a + DH // 2], g, ALU.mult)
                last.then_inc(tabs_ready, 1)
                with pool.Fori(0, NB) as s:
                    i = l * NB + s
                    for part, t, k in order:
                        if part == "in":
                            pool.wait_ge(h_ready, i + 1)
                            pool.wait_ge(hmid_ready, TPS * i + t + 1)
                            nc.gpsimd.tensor_copy(h_in[:, t, :], h[:, s * TPS + t, :]).then_inc(hin_ready, 1)
                        elif part == "qkv" and k < 4:
                            pool.wait_ge(w_ready, CREDIT + 4 * TPS * i + 4 * t + k + 1)
                            nc.gpsimd.tensor_tensor(qk[:, k, :], qk[:, k, :], swap[:, k % 2, :],
                                                    ALU.add).then_inc(rot_ready, 1)
                        elif part in ("nq", "nk"):
                            n = part == "nk"
                            pool.wait_ge(ssm_ready, 2 * TPS * i + 2 * t + n + 1)
                            nc.gpsimd.tensor_tensor(rn[:, int(n), :], ssm[:, int(n), :], minus_half[:],
                                                    ALU.pow).then_inc(rn_ready, 1)
                        elif part == "ffn":
                            pool.wait_ge(hmid_ready, TPS * i + 2 * TPS)
                            pool.wait_ge(wf_loaded, N_WF * l + N_WF)
                            nc.gpsimd.tensor_tensor(hb[:], h_mid[:], b2[:].unsqueeze(1).broadcast_to([P, TPS, C]),
                                                    ALU.add).then_inc(hb_ready, 1)
                            pool.wait_ge(fve_ready, i + 1)
                            nc.gpsimd.tensor_tensor(frstd[:], fve[:], minus_half[:, 0:TPS],
                                                    ALU.pow).then_inc(frstd_ready, 1)

        @block.scalar
        def _(act):
            act.wait_ge(ready0, 1)
            with act.Fori(0, STEPS) as i:
                def evac(n, dst, src, done):
                    nc.scalar.activation(dst, src, ACT.Copy).then_inc(done, 1)

                for part, t, k in order:
                    g = TPS * i + t
                    if part == "in":
                        act.wait_ge(hT_ps, g + 1)
                        nc.scalar.activation(xs[0:64, P * t:P * (t + 1)], M[0:64, 0:P], ACT.Copy)
                        nc.scalar.activation(xs[64:128, P * t + 1:P * (t + 1) + 1], M[64:128, 0:P],
                                             ACT.Copy).then_inc(xs_ready, 1)
                        act.wait_ge(xs_ready, g + 1)
                        act.sem_inc(m_free, 1)
                    elif part == "qkv" and k < 4:
                        act.wait_ge(qkv_ps, 6 * TPS * i + 6 * t + k + 1)
                        act.wait_ge(ss_ready[k % 2], CREDIT + 2 * TPS * i + 2 * t + k // 2)
                        nc.scalar.activation(sq[:, k % 2, :], QKV[k % 2][:, :], ACT.Square).then_inc(sq_ready, 1)
                    elif part == "qkv":
                        act.wait_ge(qkv_ps, 6 * TPS * i + 6 * t + k + 1)
                        nc.scalar.activation(v[:, t, 8 * (k - 4):8 * (k - 3), 0:DH], heads8(QKV[k % 2][:, :]),
                                             ACT.Copy).then_inc(qkv_free[k % 2], 1)
                    elif part == "rot":
                        n = t_use[part, t, k]
                        act.wait_ge(qk_ps, 4 * TPS * i + 4 * t + k + 1)
                        src = T[n % 2][:, :].rearrange("p (a x) -> p a x", x=P)
                        if k < 2:
                            nc.scalar.activation(qT[:, t, 4 * k:4 * k + 4, :], src, ACT.Copy).then_inc(t_free[n % 2], 1)
                        else:
                            a = 4 * (k - 2)
                            main = nc.scalar.activation(kT[:, t, a:a + 4, WIN:KEYS], src, ACT.Copy)
                            if t < TPS - 1:
                                main = nc.scalar.activation(kT[:, t + 1, a:a + 4, 0:WIN], src[:, :, P - WIN:P],
                                                            ACT.Copy)
                            main.then_inc(t_free[n % 2], 1)
                    elif part == "s":
                        lo = 0 if t else WIN
                        act.wait_ge(nb_ready, PAIRS * TPS * i + PAIRS * t + k + 1)
                        for hh, hd in enumerate(unit_heads(k)):
                            last = nc.scalar.activation(pr[:, hd, lo:KEYS], S[k % 2][:, hh * KEYS + lo:(hh + 1) * KEYS],
                                                        ACT.Exp, bias=nb[:, hd:hd + 1], scale=rq8[:, t, hd:hd + 1])
                        last.then_inc(s_free[k % 2], 1)
                    elif part == "pt":
                        n = t_use[part, t, k]
                        act.wait_ge(pT_ps, 4 * TPS * i + 4 * t + k + 1)
                        nc.scalar.activation(prT[:, k % 2, :, :], T[n % 2][:, :].rearrange("p (a x) -> p a x", x=P),
                                             ACT.Copy).then_inc(t_free[n % 2], 1)
                    elif part == "ot":
                        n = t_use[part, t, k]
                        act.wait_ge(oT_ps, 2 * TPS * i + 2 * t + k + 1)
                        nc.scalar.activation(oT[:, 4 * k:4 * k + 4, :], T[n % 2][:, :].rearrange("p (a x) -> p a x", x=P),
                                             ACT.Copy).then_inc(t_free[n % 2], 1)
                    elif part == "ffn":
                        act.wait_ge(xnT_ps, i + 1)
                        nc.scalar.activation(xnT[:], M[:, :], ACT.Identity, bias=ln_b[:, 0:1],
                                             scale=ln_g[:, 0:1]).then_inc(m_free, 1)
                        for c, (_, n) in enumerate(FCH):
                            act.wait_ge(gate_ps, len(FCH) * i + c + 1)
                            nc.scalar.activation(gate[0:n, c % 2, :], S[0][0:n, :], ACT.Gelu,
                                                 bias=b1[0:n, 1, c:c + 1]).then_inc(s_free[0], 1)

        @block.vector
        def _(dve):
            for sm in (m_free, o_free, w_ready, *t_free, *s_free, *qkv_free, *ss_ready):
                dve.sem_inc(sm, CREDIT)
            nc.vector.memset(xs[:, 0:1], 0.0)
            nc.vector.memset(v[:, :, :, DH:DH + 1], 1.0)
            nc.vector.memset(h_mid[:], 0.0).then_inc(ready0, 1)
            dve.wait_ge(ready0, 1)
            dve.sem_inc(hmid_ready, TPS)
            dve.sem_inc(h_ready, NB)
            with dve.Fori(0, DEPTH) as l:
                with dve.Fori(0, NB) as s:
                    i = l * NB + s
                    for part, t, k in order:
                        g = TPS * i + t
                        if part == "qkv" and k < 4:
                            n = 4 * TPS * i + 4 * t + k
                            src = heads8(QKV[k % 2][:, :])
                            cos = tabs[:, t, 2 * (k // 2), :].unsqueeze(1).broadcast_to([P, 8, DH])
                            if t == 0 and k == 0:
                                dve.wait_ge(tabs_ready, l + 1)
                            dve.wait_ge(sq_ready, n + 1)
                            nc.vector.tensor_tensor(heads8(qk[:, k, :]), src, cos, ALU.mult)
                            if k >= 2:
                                dve.wait_ge(rot_ready, n - 1)
                            for a, b in ((0, DH // 2), (DH // 2, 0)):
                                sn = tabs[:, t, 2 * (k // 2) + 1, a:a + DH // 2].unsqueeze(1).broadcast_to(
                                    [P, 8, DH // 2])
                                last = nc.vector.tensor_tensor(heads8(swap[:, k % 2, :])[:, :, a:a + DH // 2],
                                                               src[:, :, b:b + DH // 2], sn, ALU.mult)
                            last.then_inc(w_ready, 1)
                            nc.vector.tensor_reduce(ss[:, k // 2, 8 * (k % 2):8 * (k % 2) + 8],
                                                    heads8(sq[:, k % 2, :]), AX, ALU.add).then_inc(ss_ready[k % 2], 1)
                            dve.wait_ge(w_ready, CREDIT + n + 1)
                            dve.sem_inc(qkv_free[k % 2], 1)
                        elif part in ("nq", "nk"):
                            n = int(part == "nk")
                            for b in range(2):
                                dve.wait_ge(ss_ready[b], CREDIT + 2 * TPS * i + 2 * t + n + 1)
                            nc.vector.tensor_scalar(ssm[:, n, :], ss[:, n, :], 1e-24, None,
                                                    ALU.max).then_inc(ssm_ready, 1)
                            dve.wait_ge(rn_ready, 2 * TPS * i + 2 * t + n + 1)
                            if n == 0:
                                nc.vector.tensor_scalar(rq8[:, t, :], rn[:, 0, :], QK_SCALE, None, ALU.mult)
                                nc.vector.tensor_scalar(nrq8[:, t, :], rn[:, 0, :], -QK_SCALE, None,
                                                        ALU.mult).then_inc(rq_ready, 1)
                            else:
                                for c in range(2, 4):
                                    dve.wait_ge(rot_ready, 4 * TPS * i + 4 * t + c + 1)
                                    r = rn[:, 1, 8 * (c - 2):8 * (c - 1)].unsqueeze(2).broadcast_to([P, 8, DH])
                                    nc.vector.tensor_tensor(heads8(qk[:, c, :]), heads8(qk[:, c, :]), r,
                                                            ALU.mult).then_inc(kn_ready, 1)
                        elif part == "s":
                            lo = 0 if t else WIN
                            n = PAIRS * TPS * i + PAIRS * t + k
                            dve.wait_ge(s_ps, n + 1)
                            if k == 0:
                                dve.wait_ge(rq_ready, g + 1)
                            sv = S[k % 2][:, 0:2 * KEYS].rearrange("p (h x) -> p h x", x=KEYS)[:, :, lo:KEYS]
                            hs = slice(unit_heads(k)[0], unit_heads(k)[1] + 1, 2)
                            nc.vector.tensor_reduce(mx[:, hs], sv, AX, ALU.max).then_inc(mx_ready, 1)
                            dve.wait_ge(mx_ready, n + 1)
                            nc.vector.tensor_tensor(nb[:, hs], mx[:, hs], nrq8[:, t, hs],
                                                    ALU.mult).then_inc(nb_ready, 1)
                        elif part == "pt":
                            if t:
                                for b in range(2):
                                    dve.wait_ge(s_free[b], CREDIT + S_PER * i + PAIRS // 2 * t + k + 1)
                                nc.vector.transpose(ppT[96:128, 4 * k:4 * k + 4, :],
                                                    pr[0:WIN, 4 * k:4 * k + 4, 0:WIN]).then_inc(ppT_ready, 1)
                        elif part == "pv":
                            n = 4 * TPS * i + 4 * t + k
                            ov = O[:, 0:4 * (DH + 1)].rearrange("p (h x) -> p h x", x=DH + 1)
                            dve.wait_ge(pv_ps, n + 1)
                            nc.vector.reciprocal(rden[:, :], ov[:, :, DH]).then_inc(rden_ready, 1)
                            dve.wait_ge(rden_ready, n + 1)
                            nc.vector.tensor_tensor(on[:, 4 * k:4 * k + 4, :], ov[:, :, 0:DH],
                                                    rden[:, :].unsqueeze(2).broadcast_to([P, 4, DH]),
                                                    ALU.mult).then_inc(o_free, 1)
                        elif part == "wo":
                            dve.wait_ge(wo_ps, g + 1)
                            nc.vector.tensor_tensor(h_mid[:, t, :], h_in[:, t, :], M[:, 0:C],
                                                    ALU.add).then_inc(hmid_ready, 1)
                            dve.wait_ge(hmid_ready, g + TPS + 1)
                            dve.sem_inc(m_free, 1)
                        elif part == "ffn":
                            dve.wait_ge(sh_ps, i + 1)
                            sh = M[:, 0:TPS * 64].rearrange("p (t x) -> p t x", x=64)
                            for u in range(TPS):
                                nc.vector.bn_stats(fstats[:, u, 0, :], h_mid[:, u, 0:64]).then_inc(fst_ready, 1)
                                nc.vector.bn_stats(fstats[:, u, 1, :], sh[:, u, :]).then_inc(fst_ready, 1)
                            for u in range(TPS):
                                dve.wait_ge(fst_ready, 2 * TPS * i + 2 * u + 2)
                                dve.nop(nofuse=True)
                                nc.vector.bn_aggr(fmv[:, u, :], fstats[:, u, :, :].rearrange("p a b -> p (a b)")
                                                  ).then_inc(fmv_ready, 1)
                            dve.wait_ge(fmv_ready, TPS * i + TPS)
                            nc.vector.tensor_scalar(fve[:], fmv[:, :, 1], EPS, None, ALU.add).then_inc(fve_ready, 1)
                            dve.wait_ge(frstd_ready, i + 1)
                            for u in range(TPS):
                                nc.vector.tensor_scalar(xn[:, u, 0:64], h_mid[:, u, 0:64], fmv[:, u, 0:1],
                                                        frstd[:, u:u + 1], ALU.subtract, ALU.mult)
                                nc.vector.tensor_scalar(xn[:, u, 64:128], sh[:, u, :], fmv[:, u, 0:1],
                                                        frstd[:, u:u + 1], ALU.subtract, ALU.mult
                                                        ).then_inc(xn_ready, 1)
                            dve.wait_ge(xn_ready, TPS * i + TPS)
                            dve.sem_inc(m_free, 1)
                            for c, (_, n) in enumerate(FCH):
                                dve.wait_ge(lin_ps, len(FCH) * i + c + 1)
                                dve.wait_ge(s_free[0], CREDIT + S_PER * i + S_PER - len(FCH) + c + 1)
                                nc.vector.scalar_tensor_tensor(out=uT[0:n, c, :], in0=S[1][0:n, :],
                                                               scalar=b1[0:n, 0, c:c + 1], in1=gate[0:n, c % 2, :],
                                                               op0=ALU.add, op1=ALU.mult).then_inc(s_free[1], 1)
                            dve.wait_ge(y_ps, i + 1)
                            dve.wait_ge(hb_ready, i + 1)
                            nc.vector.tensor_tensor(h[:, bass.ds(s * TPS, TPS), :], hb[:],
                                                    M[:, :].rearrange("p (t c) -> p t c", c=C),
                                                    ALU.add).then_inc(h_ready, 1)
                            dve.wait_ge(h_ready, i + NB + 1)
                            dve.sem_inc(m_free, 1)

        @block.tensor
        def _(pe):
            def t_wait(i, n):
                pe.wait_ge(t_free[n % 2], CREDIT + T_PER // 2 * i + n // 2)

            pe.wait_ge(ready0, 1)
            with pe.Fori(0, DEPTH) as l:
                with pe.Fori(0, NB) as s:
                    i = l * NB + s
                    for part, t, k in order:
                        g = TPS * i + t
                        if part == "in":
                            pe.wait_ge(hin_ready, g + 1)
                            pe.wait_ge(m_free, CREDIT + M_PER * i + m_use[part, t, k])
                            nc.tensor.transpose(M[:, 0:P], h_in[:, t, :], ident).then_inc(hT_ps, 1)
                        elif part == "qkv":
                            if k == 0:
                                pe.wait_ge(xs_ready, g + 1)
                                if t == 0:
                                    pe.wait_ge(wqkv_loaded, 16 * l + 16)
                            pe.wait_ge(qkv_free[k % 2], CREDIT + 3 * TPS * i + 3 * t + k // 2)
                            nc.tensor.matmul(QKV[k % 2][:, :], xs[:, P * t:P * (t + 1)],
                                             wqkv[:, l % 2, CH * k:CH * (k + 1)], start=True, stop=True
                                             ).then_inc(qkv_ps, 1)
                        elif part == "rot":
                            n = t_use[part, t, k]
                            t_wait(i, n)
                            if k < 2:
                                pe.wait_ge(rot_ready, 4 * TPS * i + 4 * t + k + 1)
                            else:
                                pe.wait_ge(kn_ready, 2 * TPS * i + 2 * t + k - 1)
                            for a in range(4):
                                last = nc.tensor.transpose(T[n % 2][:, P * a:P * (a + 1)],
                                                           qk[:, k, P * a:P * (a + 1)], ident)
                            last.then_inc(qk_ps, 1)
                        elif part == "s":
                            lo = 0 if t else WIN
                            if k == 0:
                                for b in range(2):
                                    done = max(n // 2 + 1 for n in (t_use["rot", t, j] for j in range(4)) if n % 2 == b)
                                    pe.wait_ge(t_free[b], CREDIT + T_PER // 2 * i + done)
                            pe.wait_ge(s_free[k % 2], CREDIT + S_PER * i + PAIRS // 2 * t + k // 2)
                            sv = S[k % 2][:, 0:2 * KEYS].rearrange("p (h x) -> p h x", x=KEYS)
                            nc.tensor.matmul(sv[:, :, lo:KEYS], const["ident_bf"], const["mask"][:, :, lo:KEYS],
                                             start=True, stop=False, skip_group_check=True)
                            r = slice(DH * (k % 2), DH * (k % 2) + DH)
                            for hh, hd in enumerate(unit_heads(k)):
                                last = nc.tensor.matmul(sv[:, hh, lo:KEYS], qT[r, t, hd // 2, :],
                                                        kT[r, t, hd // 2, lo:KEYS],
                                                        start=False, stop=True, skip_group_check=True)
                            last.then_inc(s_ps, 1)
                        elif part == "pt":
                            n = t_use[part, t, k]
                            t_wait(i, n)
                            for b in range(2):
                                pe.wait_ge(s_free[b], CREDIT + S_PER * i + PAIRS // 2 * t + k + 1)
                            for a in range(4):
                                last = nc.tensor.transpose(T[n % 2][:, P * a:P * (a + 1)],
                                                           pr[:, 4 * k + a, WIN:KEYS], ident)
                            last.then_inc(pT_ps, 1)
                        elif part == "pv":
                            n = t_use["pt", t, k]
                            pe.wait_ge(t_free[n % 2], CREDIT + T_PER // 2 * i + n // 2 + 1)
                            if k == 0:
                                for b in range(2):
                                    pe.wait_ge(qkv_free[b], CREDIT + 3 * TPS * i + 3 * t + 3)
                            if t:
                                pe.wait_ge(ppT_ready, 4 * (TPS - 1) * i + 4 * (t - 1) + k + 1)
                            pe.wait_ge(o_free, CREDIT + 4 * TPS * i + 4 * t + k)
                            for a in range(4):
                                hd = 4 * k + a
                                o = O[:, a * (DH + 1):(a + 1) * (DH + 1)]
                                last = nc.tensor.matmul(o, prT[:, k % 2, a, :], v[:, t, hd, :], start=True,
                                                        stop=not t, skip_group_check=True)
                                if t:
                                    last = nc.tensor.matmul(O[0:WIN, a * (DH + 1):(a + 1) * (DH + 1)],
                                                            ppT[96:128, hd, :], v[96:128, t - 1, hd, :], start=False,
                                                            stop=True, skip_group_check=True)
                            last.then_inc(pv_ps, 1)
                        elif part == "ot":
                            n = t_use[part, t, k]
                            t_wait(i, n)
                            pe.wait_ge(o_free, CREDIT + 4 * TPS * i + 4 * t + 2 * k + 2)
                            for a in range(4):
                                hd = 8 * k + 2 * a
                                last = nc.tensor.transpose(T[n % 2][:, P * a:P * (a + 1)],
                                                           on[:, hd:hd + 2, :].rearrange("p a b -> p (a b)"), ident)
                            last.then_inc(oT_ps, 1)
                        elif part == "wo":
                            for j in range(2):
                                n = t_use["ot", t, j]
                                pe.wait_ge(t_free[n % 2], CREDIT + T_PER // 2 * i + n // 2 + 1)
                            if t == 0:
                                pe.wait_ge(wo_loaded, 16 * l + 16)
                            pe.wait_ge(m_free, CREDIT + M_PER * i + m_use[part, t, k])
                            for c in range(PAIRS):
                                last = nc.tensor.matmul(M[:, 0:C], oT[:, c, :], wo[:, c, :], start=(c == 0),
                                                        stop=(c == PAIRS - 1))
                            last.then_inc(wo_ps, 1)
                        elif part == "ffn":
                            m0 = m_use[part, t, k]
                            pe.wait_ge(hmid_ready, TPS * i + 2 * TPS)
                            pe.wait_ge(m_free, CREDIT + M_PER * i + m0)
                            nc.tensor.matmul(M[:, 0:TPS * 64], down, h_mid[:, :, 64:128], start=True, stop=False,
                                             skip_group_check=True)
                            nc.tensor.matmul(M[:, 64:TPS * 64], carry, h_mid[:, 0:TPS - 1, 64:128], start=False,
                                             stop=True, skip_group_check=True).then_inc(sh_ps, 1)
                            pe.wait_ge(m_free, CREDIT + M_PER * i + m0 + 1)
                            for u in range(TPS):
                                last = nc.tensor.transpose(M[:, P * u:P * (u + 1)], xn[:, u, :], ident)
                            last.then_inc(xnT_ps, 1)
                            pe.wait_ge(m_free, CREDIT + M_PER * i + m0 + 2)
                            pe.wait_ge(wf_loaded, N_WF * l + N_WF)
                            for c, (r0, n) in enumerate(FCH):
                                for a, done in ((1, gate_ps), (0, lin_ps)):
                                    pe.wait_ge(s_free[1 - a], CREDIT + S_PER * i + S_PER - len(FCH) + c)
                                    nc.tensor.matmul(S[1 - a][0:n, :], w1[:, a * DI + r0:a * DI + r0 + n], xnT[:],
                                                     start=True, stop=True).then_inc(done, 1)
                            pe.wait_ge(s_free[1], CREDIT + S_PER * i + S_PER)
                            for u in range(TPS):
                                for c, (_, n) in enumerate(FCH):
                                    last = nc.tensor.matmul(M[:, C * u:C * (u + 1)], uT[0:n, c, P * u:P * (u + 1)],
                                                            w2[0:n, c, :], start=(c == 0), stop=(c == len(FCH) - 1))
                            last.then_inc(y_ps, 1)


def alibi_phase(nc, x, h, const, w):
    units = TPS * H2
    GR = H2 // 4
    TABW = 2 * NT - P
    slopes = alibi_slopes()
    LAG_T, LAG_PV, LAG_ON, LAG_WP = 2, 3, 6, 8

    with ExitStack() as ctx:
        def sb(n, shape, dt=F32):
            return ctx.enter_context(nc.sbuf_tensor(f"al_{n}", shape, dt))

        def ps(n):
            return ctx.enter_context(nc.psum_tensor(f"al_{n}", [P, 512], F32))

        sem = ctx.enter_context(phase_semaphores(nc, "al"))

        wraw = sb("wraw", [P, 3 * C])
        wpad = sb("wpad", [P, 2, GR, 4, 32])
        bpad = sb("bpad", [P, 2, GR])
        bqs = sb("bqs", [P, GR])
        bv, bo = sb("bv", [P, C]), sb("bo", [P, C])
        wp = sb("wp", [P, C])
        dist = sb("dist", [P, TABW])
        tab = sb("tab", [P, H2, TABW])
        z = sb("z", [P, TPS, C])
        zT = sb("zT", [P, NT])
        qkT = sb("qkT", [P, 2 * GR, NT])
        v = sb("v", [P, TPS, H2, D2 + 1])
        sc = sb("sc", [P, 2, NT])
        nm = sb("nm", [P, units])
        pr = sb("pr", [P, 2, NT])
        prT = sb("prT", [P, 2, NT])
        rden = sb("rden", [P, H2])
        on = sb("on", [P, H2, D2])
        onT = sb("onT", [P, P])
        S = [ps("psS0"), ps("psS1")]
        T = [ps("psT0"), ps("psT1")]
        A = [ps("psA0"), ps("psA1")]
        M, N = ps("psM"), ps("psN")

        (loaded, zeroed, pad_ready, tab_ready, ones_ready, xb_ready, z_ready, zT_ps, zT_ready, v_ps, v_ready,
         s_ps, sc_ready, exp_ready, pT_ps, pv_ps, rden_ready, on_ready, onT_ps, onT_ready, y_ps, x_done,
         v_zero) = [sem(n) for n in (
             "loaded", "zeroed", "pad_ready", "tab_ready", "ones_ready", "xb_ready", "z_ready", "zT_ps",
             "zT_ready", "v_ps", "v_ready", "s_ps", "sc_ready", "exp_ready", "pT_ps", "pv_ps", "rden_ready",
             "on_ready", "onT_ps", "onT_ready", "y_ps", "x_done", "v_zero")]
        qk_ps = sem("qk_ps")
        qk_ready = [sem("qk_ready0"), sem("qk_ready1")]
        pT_ready = [sem("pT_ready0"), sem("pT_ready1")]
        block = ctx.enter_context(nc.Block())
        ident = const["ident"]
        N_LOAD = 16 * (5 + 8)

        @block.sync
        def _(sp):
            sp.dma_start(wraw[:], w["W_qkv"][:, :]).then_inc(loaded, 16)
            sp.dma_start(wp[:], w["W_proj"][:, :]).then_inc(loaded, 16)
            sp.dma_start(bv[:], w["b_qkv"][2 * C:3 * C].partition_broadcast(P)).then_inc(loaded, 16)
            sp.dma_start(bo[:], w["b_proj"][:].partition_broadcast(P)).then_inc(loaded, 16)
            sp.dma_start(dist[:], w["dist"][:, :]).then_inc(loaded, 16)
            sp.wait_ge(zeroed, 1)
            for n in range(2):
                src = w["b_qkv"][n * C:(n + 1) * C].rearrange("(c j d) -> j d c", j=4, d=D2)
                for j in range(4):
                    sp.dma_start(bpad[32 * j:32 * j + D2, n, :], src[j], allow_slow_non_contiguous=True).then_inc(loaded, 16)

        @block.gpsimd
        def _(pool):
            pool.wait_ge(zeroed, 1)
            pool.wait_ge(loaded, N_LOAD)
            nc.gpsimd.tensor_tensor(x[:], x[:], bo[:].unsqueeze(1).broadcast_to([P, TILES, C]),
                                    ALU.add).then_inc(xb_ready, 1)
            with pool.Fori(0, NB) as b:
                pool.wait_ge(zT_ps, CREDIT + b)
                nc.gpsimd.tensor_copy(z[:], h[:, bass.ds(b * TPS, TPS), :]).then_inc(z_ready, 1)

        @block.scalar
        def _(act):
            act.wait_ge(pad_ready, 1)
            with act.Fori(0, NB) as b:
                act.wait_ge(zT_ps, CREDIT + b + 1)
                nc.scalar.activation(zT[:], M[:, :], ACT.Copy).then_inc(zT_ready, 1)
                for c in range(2 * GR):
                    act.wait_ge(qk_ps, 2 * GR * b + c + 1)
                    if c < GR:
                        nc.scalar.activation(qkT[:, c, :], A[c % 2][:, :], ACT.Identity, bias=bqs[:, c:c + 1],
                                             scale=float(D2) ** -0.5).then_inc(qk_ready[c % 2], 1)
                    else:
                        nc.scalar.activation(qkT[:, c, :], A[c % 2][:, :], ACT.Identity,
                                             bias=bpad[:, 1, c - GR:c - GR + 1]).then_inc(qk_ready[c % 2], 1)
                for k in range(units + LAG_WP + 1):
                    if k < units:
                        act.wait_ge(sc_ready, CREDIT + units * b + k + 1)
                        if k >= 2:
                            act.wait_ge(pT_ps, units * b + k - 1)
                        nc.scalar.activation(pr[:, k % 2, :], sc[:, k % 2, :], ACT.Exp, bias=nm[:, k:k + 1],
                                             scale=-1.0).then_inc(exp_ready, 1)
                    u = k - LAG_T
                    if 0 <= u < units and u % 2 == 0:
                        act.wait_ge(pT_ps, units * b + u + 1)
                        nc.scalar.activation(prT[:, 0, :], T[0][:, :], ACT.Copy).then_inc(pT_ready[0], 1)
                    if k >= H2 + LAG_ON and (k - LAG_ON) % H2 == 0:
                        qt = (k - LAG_ON) // H2 - 1
                        act.wait_ge(onT_ps, TPS * b + qt + 1)
                        nc.scalar.activation(onT[:], M[:, 0:P], ACT.Copy).then_inc(onT_ready, 1)

        @block.vector
        def _(dve):
            for sm in (zT_ps, exp_ready, onT_ready, on_ready, x_done, sc_ready, *qk_ready, *pT_ready):
                dve.sem_inc(sm, CREDIT)
            nc.vector.memset(wpad[:], 0.0)
            nc.vector.memset(bpad[:], 0.0)
            nc.vector.memset(v[:, :, :, D2:D2 + 1], 1.0).then_inc(zeroed, 1)
            dve.wait_ge(zeroed, 1)
            dve.wait_ge(loaded, N_LOAD)
            for n in range(2):
                nc.vector.tensor_copy(wpad[:, n, :, :, 0:D2],
                                      wraw[:, n * C:(n + 1) * C].rearrange("p (c j d) -> p c j d", j=4, d=D2))
            nc.vector.tensor_scalar(bqs[:], bpad[:, 0, :], float(D2) ** -0.5, None, ALU.mult).then_inc(pad_ready, 1)
            for hd in range(H2):
                nc.vector.tensor_scalar(tab[:, hd, :], dist[:], slopes[hd], None, ALU.mult).then_inc(tab_ready, 1)
            dve.wait_ge(tab_ready, H2)
            with dve.Fori(0, NB) as b:
                dve.wait_ge(v_ps, b + 1)
                nc.vector.tensor_tensor(v[:, :, :, 0:D2], N[:, :].rearrange("p (t h d) -> p t h d", h=H2, d=D2),
                                        bv[:].rearrange("p (h d) -> p h d", d=D2).unsqueeze(1).broadcast_to(
                                            [P, TPS, H2, D2]), ALU.add).then_inc(v_ready, 1)
                for k in range(units + LAG_WP + 1):
                    if k < units:
                        qt, hd = k // H2, k % H2
                        dve.wait_ge(s_ps, units * b + k + 1)
                        dve.wait_ge(exp_ready, CREDIT + units * b + k - 1) if k >= 2 else dve.wait_ge(exp_ready, CREDIT + units * b)
                        off = NT - P - P * qt
                        dve.nop(nofuse=True)
                        nc.vector.tensor_tensor_reduce(sc[:, k % 2, :], S[k % 2][:, :], tab[:, hd, off:off + NT],
                                                       -1.0, 0.0, ALU.add, ALU.min, nm[:, k:k + 1]
                                                       ).then_inc(sc_ready, 1)
                    u = k - LAG_T
                    if 0 <= u < units and u % 2:
                        dve.wait_ge(pT_ps, units * b + u + 1)
                        nc.vector.tensor_copy(prT[:, 1, :], T[1][:, :]).then_inc(pT_ready[1], 1)
                    if k >= H2 + LAG_PV and (k - LAG_PV) % H2 == 0:
                        qt = (k - LAG_PV) // H2 - 1
                        ov = A[qt % 2][:, 0:H2 * (D2 + 1)].rearrange("p (h x) -> p h x", x=D2 + 1)
                        dve.wait_ge(pv_ps, units * b + H2 * qt + H2)
                        nc.vector.reciprocal(rden[:], ov[:, :, D2]).then_inc(rden_ready, 1)
                        dve.wait_ge(rden_ready, TPS * b + qt + 1)
                        nc.vector.tensor_tensor(on[:], ov[:, :, 0:D2], rden[:].unsqueeze(2).broadcast_to([P, H2, D2]),
                                                ALU.mult).then_inc(on_ready, 1)
                    if k >= H2 + LAG_WP and (k - LAG_WP) % H2 == 0:
                        qt = (k - LAG_WP) // H2 - 1
                        dve.wait_ge(y_ps, TPS * b + qt + 1)
                        dve.wait_ge(xb_ready, 1)
                        nc.vector.tensor_tensor(x[:, b * TPS + qt, :], x[:, b * TPS + qt, :], N[:, 0:C],
                                                ALU.add).then_inc(x_done, 1)

        @block.tensor
        def _(pe):
            pe.wait_ge(pad_ready, 1)
            pe.wait_ge(zeroed, 1)
            pe.wait_ge(loaded, N_LOAD)
            with pe.Fori(0, NB) as b:
                pe.wait_ge(z_ready, b + 1)
                pe.wait_ge(onT_ready, CREDIT + TPS * b)
                for t in range(TPS):
                    last = nc.tensor.transpose(M[:, P * t:P * (t + 1)], z[:, t, :], ident)
                last.then_inc(zT_ps, 1)
                pe.wait_ge(zT_ready, b + 1)
                pe.wait_ge(on_ready, CREDIT + TPS * b)
                for c in range(2 * GR):
                    pe.wait_ge(qk_ready[c % 2], CREDIT + GR * b + c // 2)
                    nc.tensor.matmul(A[c % 2][:, :], wpad[:, c // GR, c % GR, :, :].rearrange("p j d -> p (j d)"),
                                     zT[:], start=True, stop=True).then_inc(qk_ps, 1)
                pe.wait_ge(x_done, CREDIT + TPS * b)
                for t in range(TPS):
                    last = nc.tensor.matmul(N[:, C * t:C * (t + 1)], zT[:, P * t:P * (t + 1)], wraw[:, 2 * C:3 * C],
                                            start=True, stop=True)
                last.then_inc(v_ps, 1)
                for q in qk_ready:
                    pe.wait_ge(q, CREDIT + GR * b + GR)
                pe.wait_ge(v_ready, b + 1)
                for k in range(units + LAG_WP + 1):
                    if k < units:
                        qt, hd = k // H2, k % H2
                        c, j = hd // 4, 32 * (hd % 4)
                        if k >= 2:
                            pe.wait_ge(sc_ready, CREDIT + units * b + k - 1)
                        else:
                            pe.wait_ge(sc_ready, CREDIT + units * b)
                        nc.tensor.matmul(S[k % 2][:, :], qkT[j:j + D2, c, P * qt:P * (qt + 1)],
                                         qkT[j:j + D2, GR + c, :], start=True, stop=True).then_inc(s_ps, 1)
                    u = k - LAG_T
                    if 0 <= u < units:
                        pe.wait_ge(exp_ready, CREDIT + units * b + u + 1)
                        pe.wait_ge(pT_ready[u % 2], CREDIT + units // 2 * b + u // 2)
                        for a in range(TPS):
                            last = nc.tensor.transpose(T[u % 2][:, P * a:P * (a + 1)],
                                                       pr[:, u % 2, P * a:P * (a + 1)], ident)
                        last.then_inc(pT_ps, 1)
                    u = k - LAG_PV
                    if 0 <= u < units:
                        qt, hd = u // H2, u % H2
                        pe.wait_ge(pT_ready[u % 2], CREDIT + units // 2 * b + u // 2 + 1)
                        if hd == 0 and qt >= 2:
                            pe.wait_ge(on_ready, CREDIT + TPS * b + qt - 1)
                        for a in range(TPS):
                            last = nc.tensor.matmul(A[qt % 2][:, hd * (D2 + 1):(hd + 1) * (D2 + 1)],
                                                    prT[:, u % 2, P * a:P * (a + 1)], v[:, a, hd, :],
                                                    start=(a == 0), stop=(a == TPS - 1), skip_group_check=True)
                        last.then_inc(pv_ps, 1)
                    if k >= H2 + LAG_ON and (k - LAG_ON) % H2 == 0:
                        qt = (k - LAG_ON) // H2 - 1
                        pe.wait_ge(on_ready, CREDIT + TPS * b + qt + 1)
                        pe.wait_ge(onT_ready, CREDIT + TPS * b + qt)
                        nc.tensor.transpose(M[:, 0:P], on[:].rearrange("p h d -> p (h d)"), ident).then_inc(onT_ps, 1)
                    if k >= H2 + LAG_WP and (k - LAG_WP) % H2 == 0:
                        qt = (k - LAG_WP) // H2 - 1
                        pe.wait_ge(onT_ready, CREDIT + TPS * b + qt + 1)
                        pe.wait_ge(x_done, CREDIT + TPS * b + qt)
                        nc.tensor.matmul(N[:, 0:C], onT[:], wp[:], start=True, stop=True).then_inc(y_ps, 1)


def build(nc, ins, out):
    with ExitStack() as ctx:
        def sb(n, shape, dt=F32):
            return ctx.enter_context(nc.sbuf_tensor(n, shape, dt))

        def constant(name, array, dt=F32):
            return nc.inline_tensor(np.ascontiguousarray(array), name).ap()

        eye3 = sb("eye3", [P, 3 * P])
        ident_bf = sb("ident_bf", [P, P], BF16)
        mask_f = sb("mask_f", [P, 2, KEYS])
        mask = sb("mask", [P, 2, KEYS], BF16)
        rotary = sb("rotary", [P, TPS, 4, DH])
        x = sb("x", [P, TILES, C])
        h = sb("h", [P, TILES, C])
        c_eye = constant("c_eye3", shift_matrices())
        c_mask = constant("c_mask", window_mask().astype(np.float32))
        c_rot = constant("c_rotary", rotary_constants())
        d = np.arange(2 * NT - P)[None, :] - (NT - P) - np.arange(P)[:, None]
        c_dist = constant("c_dist", np.minimum(d, 0).astype(np.float32))
        const = {"ident": eye3[:, 0:P], "down": eye3[:, P:2 * P], "carry": eye3[:, 2 * P:3 * P],
                 "ident_bf": ident_bf[:], "mask": mask[:], "rotary": rotary[:]}
        with ExitStack() as c2:
            got = c2.enter_context(nc.semaphore("const_loaded"))
            made = c2.enter_context(nc.semaphore("const_made"))
            block = c2.enter_context(nc.Block())

            @block.sync
            def _(sp):
                sp.dma_start(eye3[:], c_eye).then_inc(got, 16)
                sp.dma_start(mask_f[:], c_mask).then_inc(got, 16)
                sp.dma_start(rotary[:], c_rot).then_inc(got, 16)

            @block.vector
            def _(dve):
                dve.wait_ge(got, 48)
                nc.vector.tensor_copy(ident_bf[:], eye3[:, 0:P])
                nc.vector.tensor_copy(mask[:], mask_f[:]).then_inc(made, 1)
                dve.wait_ge(made, 1)

        f_w = {n: ins["L0_ffn_" + n] for n in ("Wqkv", "q_scale", "k_scale", "Wo", "ln_g", "ln_b", "W1", "b1",
                                               "W2", "b2")}
        a_w = {n: ins["L0_attn_" + n] for n in ("W_qkv", "b_qkv", "W_proj", "b_proj")}
        a_w["dist"] = c_dist
        layer_norm_phase(nc, "n1", x, h, ins["L0_attn_x"], None, None)
        macaron_phase(nc, "f1", h, const, f_w)
        layer_norm_phase(nc, "n2", x, h, None, 0.5, None)
        alibi_phase(nc, x, h, const, a_w)
        layer_norm_phase(nc, "n3", x, h, None, None, None)
        macaron_phase(nc, "f2", h, const, f_w)
        layer_norm_phase(nc, "end", x, h, None, 0.5, out)


_INS = ["L0_attn_x", "L0_attn_W_qkv", "L0_attn_b_qkv", "L0_attn_W_proj", "L0_attn_b_proj", "L0_ffn_Wqkv",
        "L0_ffn_q_scale", "L0_ffn_k_scale", "L0_ffn_Wo", "L0_ffn_ln_g", "L0_ffn_ln_b", "L0_ffn_W1", "L0_ffn_b1",
        "L0_ffn_W2", "L0_ffn_b2"]


def kernel(**inputs):
    import concourse.bacc as bacc
    from concourse.bass_utils import run_bass_kernel_spmd

    nc = bacc.Bacc("TRN2", target_bir_lowering=False, num_devices=1)
    arrays, ins = {}, {}
    for name in _INS:
        a = np.ascontiguousarray(inputs[name])
        arrays[f"in_{name}"] = a
        ins[name] = nc.dram_tensor(f"in_{name}", a.shape, mybir.dt.from_np(a.dtype), kind="ExternalInput").ap()
    out = nc.dram_tensor("out_x", (NB, NT, C), F32, kind="ExternalOutput").ap()
    build(nc, ins, out)
    r = run_bass_kernel_spmd(nc, [arrays], core_ids=[0])
    return r.results[0]["out_x"]
```

```python
from contextlib import ExitStack, contextmanager

import numpy as np
import concourse.bass as bass
from concourse import mybir

F32 = mybir.dt.float32
BF16 = mybir.dt.bfloat16
ALU = mybir.AluOpType
ACT = mybir.ActivationFunctionType
AX = mybir.AxisListType.X

P = 128
NB, NT, C = 4, 512, 128
TPS = NT // P
TILES = NB * TPS
DEPTH, HEADS, DH, WIN = 6, 16, 64, 32
INNER = HEADS * DH
PAIRS = HEADS // 2
KEYS = P + WIN
CH = 512
DI = C * 4 * 2 // 3
FCH = [(0, 128), (128, 128), (256, DI - 256)]
QK_SCALE = 8.0
EPS = 1e-5
MASKED = -1e30
H2, D2 = 16, 8
STEPS = DEPTH * NB
CREDIT = 1


def rotary_constants():
    f = np.float32
    half = np.arange(0, DH, 2, dtype=f)
    inv_freq = (f(1.0) / np.power(f(10000.0), half / f(DH))).astype(f)
    t = np.arange(NT, dtype=f)
    freqs = t[:, None] * inv_freq[None, :]
    freqs = np.concatenate([freqs, freqs], -1)
    base = (half + f(0.4 * DH)) / f(1.4 * DH)
    power = (t - f(NT // 2)) / f(WIN // 2)
    scale = np.power(base[None, :], power[:, None]).astype(f)
    scale = np.concatenate([scale, scale], -1)
    cos, sin = np.cos(freqs).astype(f), np.sin(freqs).astype(f)
    sin[:, :DH // 2] *= f(-1.0)
    inv = (f(1.0) / scale).astype(f)
    tabs = np.stack([cos * scale, sin * scale, cos * inv, sin * inv], 1)
    return np.ascontiguousarray(tabs.reshape(TPS, P, 4, DH).transpose(1, 0, 2, 3)).astype(f)


def window_mask():
    d = np.arange(KEYS)[None, :] - np.arange(P)[:, None]
    m = np.where((d >= 0) & (d <= WIN), 0.0, MASKED)
    return np.stack([m, m], 1)


def alibi_slopes():
    start = 2 ** (-2 ** (-(np.log2(H2) - 3)))
    return [float(start * start ** i) for i in range(H2)]


def shift_matrices():
    down, carry = np.eye(P, k=1, dtype=np.float32), np.zeros((P, P), np.float32)
    carry[P - 1, 0] = 1.0
    return np.concatenate([np.eye(P, dtype=np.float32), down, carry], 1)


@contextmanager
def phase_semaphores(nc, tag):
    made = []

    def sem(name):
        made.append(nc.alloc_semaphore(f"{tag}_{name}"))
        return made[-1]

    yield sem
    nc.clear_and_free_semaphores(made)
    nc.all_engine_barrier()


SLOTS = 8 * TPS
BACK = 10.2
FRONT_PARTS = [("in", 0, 2.0), ("qkv", 0, 3.0), ("qkv", 1, 4.0), ("qkv", 2, 4.9), ("qkv", 3, 5.8), ("qkv", 4, 6.7),
               ("qkv", 5, 7.6), ("rotate", 0, 3.6), ("rotate", 1, 4.6), ("rotate", 2, 5.5), ("rotate", 3, 6.4),
               ("norm", 0, 4.9), ("scale", 0, 6.2), ("norm", 1, 6.7), ("scale", 1, 8.3),
               ("rot", 0, 5.0), ("rot", 1, 6.0), ("rot", 2, 8.8), ("rot", 3, 9.2)]
BACK_PARTS = [("s", k, float(k)) for k in range(PAIRS)] + [
    ("pt", 0, 3.0), ("pv", 0, 4.0), ("pt", 1, 5.0), ("pv", 1, 6.0), ("pt", 2, 7.0), ("ot", 0, 7.6), ("pv", 2, 8.0),
    ("pt", 3, 9.0), ("pv", 3, 10.0), ("ot", 1, 10.6), ("wo", 0, 11.3)]
FFN_PARTS = [("shift", 0, 46.0), ("stats", 0, 46.6), ("ln", 0, 47.8), ("xnT", 0, 48.6), ("gate", 0, 50.0),
             ("gate", 1, 50.25), ("gate", 2, 50.5), ("lin", 0, 51.6), ("lin", 1, 52.4), ("lin", 2, 53.2),
             ("out", 0, 54.5)]
STEP_PARTS = ([(n, t, k, at + 8 * t) for t in range(TPS) for n, k, at in FRONT_PARTS] +
              [(n, t, k, at + 8 * t + BACK) for t in range(TPS) for n, k, at in BACK_PARTS] +
              [(n, 0, k, at) for n, k, at in FFN_PARTS])
DELAY = {"PE": {},
         "ACT": {"in": 0.2, "rot": 0.2, "qkv": 0.35, "s": 0.5, "pt": 0.25, "ot": 0.25, "gate": 0.15, "xnT": 0.2},
         "DVE": {"s": 0.3, "pv": 0.3, "wo": 0.3, "pt": 0.25, "lin": 0.3, "out": 0.5, "shift": 0.3},
         "POOL": {"in": -1.5, "rotate": 0.5, "norm": 0.2, "stats": 0.3}}
TA_USE = {("in", 0): 0, **{("rot", k): 1 + k for k in range(4)}}
TP_USE = {("pt", 0): 0, ("pt", 1): 1, ("pt", 2): 2, ("ot", 0): 3, ("pt", 3): 4, ("ot", 1): 5}
O_USE = {**{("pv", k): k for k in range(4)}, ("wo", 0): 4}
F_USE = {("shift", 0): 0, ("xnT", 0): 1, **{("gate", c): 2 + c for c in range(3)},
         **{("lin", c): 5 + c for c in range(3)}, ("out", 0): 8}


def engine_schedule(engine):
    at = [(x[3] + DELAY[engine].get(x[0], 0.0), n, x[:3]) for n, x in enumerate(STEP_PARTS)]
    assert all(0 <= y[0] < 2 * SLOTS for y in at)
    return [(part, int(y // SLOTS)) for y, n, part in sorted(at, key=lambda z: (z[0] % SLOTS, z[1]))]


def run_steps(eng, engine, emit):
    parts = engine_schedule(engine)
    for part, lag in parts:
        if lag == 0:
            emit(0, 0, part)
    with eng.Fori(1, STEPS) as j:
        layer = [eng.snap(j // NB), eng.snap((j - 1) // NB)]
        for part, lag in parts:
            emit(j - lag, layer[lag], part)
    for part, lag in parts:
        if lag == 1:
            emit(STEPS - 1, DEPTH - 1, part)


def unit_heads(k):
    return [4 * (k // 2) + k % 2, 4 * (k // 2) + k % 2 + 2]


def layer_norm_phase(nc, tag, x, h, x_in, mix, out_dram):
    with ExitStack() as ctx:
        sem = ctx.enter_context(phase_semaphores(nc, tag))
        stats = ctx.enter_context(nc.sbuf_tensor(f"{tag}_stats", [P, TILES, 6], F32))
        mv = ctx.enter_context(nc.sbuf_tensor(f"{tag}_mv", [P, TILES, 2], F32))
        ve = ctx.enter_context(nc.sbuf_tensor(f"{tag}_ve", [P, TILES], F32))
        mh = ctx.enter_context(nc.sbuf_tensor(f"{tag}_mh", [P, TILES], F32))
        rstd = ctx.enter_context(nc.sbuf_tensor(f"{tag}_rstd", [P, TILES], F32))
        x_loaded, x_ready, stats_ready, mv_ready, ve_ready, mh_ready, rstd_ready, h_ready, stored = [
            sem(n) for n in ("x_loaded", "x_ready", "stats_ready", "mv_ready", "ve_ready", "mh_ready",
                             "rstd_ready", "h_ready", "stored")]
        block = ctx.enter_context(nc.Block())

        @block.sync
        def _(sp):
            if x_in is not None:
                for b in range(NB):
                    sp.dma_start(x[:, b * TPS:(b + 1) * TPS, :],
                                 x_in[b].rearrange("(t p) c -> p t c", p=P)).then_inc(x_loaded, 16)
            if out_dram is not None:
                for b in range(NB):
                    sp.wait_ge(x_ready, b + 1)
                    sp.dma_start(out_dram[b].rearrange("(t p) c -> p t c", p=P),
                                 x[:, b * TPS:(b + 1) * TPS, :]).then_inc(stored, 16)
                sp.wait_ge(stored, 16 * NB)

        @block.vector
        def _(dve):
            if out_dram is None:
                nc.vector.memset(mh[:], -0.5).then_inc(mh_ready, 1)
            for b in range(NB):
                sl = slice(b * TPS, (b + 1) * TPS)
                if x_in is not None:
                    dve.wait_ge(x_loaded, 16 * NB)
                if mix is not None:
                    nc.vector.scalar_tensor_tensor(out=x[:, sl, :], in0=h[:, sl, :], scalar=mix, in1=x[:, sl, :],
                                                   op0=ALU.mult, op1=ALU.add).then_inc(x_ready, 1)
            if out_dram is not None:
                return
            if mix is not None:
                dve.wait_ge(x_ready, NB)
            for n in range(TILES):
                nc.vector.bn_stats(stats[:, n, :], x[:, n, :]).then_inc(stats_ready, 1)
            for n in range(TILES):
                dve.wait_ge(stats_ready, n + 1)
                nc.vector.bn_aggr(mv[:, n, :], stats[:, n, :]).then_inc(mv_ready, 1)
            dve.wait_ge(mv_ready, TILES)
            nc.vector.tensor_scalar(ve[:], mv[:, :, 1], EPS, None, ALU.add).then_inc(ve_ready, 1)
            dve.wait_ge(rstd_ready, 1)
            for n in range(TILES):
                nc.vector.tensor_scalar(h[:, n, :], x[:, n, :], mv[:, n, 0:1], rstd[:, n:n + 1],
                                        ALU.subtract, ALU.mult).then_inc(h_ready, 1)

        @block.gpsimd
        def _(pool):
            if out_dram is None:
                pool.wait_ge(mh_ready, 1)
                pool.wait_ge(ve_ready, 1)
                nc.gpsimd.tensor_tensor(rstd[:], ve[:], mh[:], ALU.pow).then_inc(rstd_ready, 1)


def macaron_phase(nc, tag, h, const, w):
    LF = len(FCH)
    with ExitStack() as ctx:
        def sb(n, shape, dt=F32):
            return ctx.enter_context(nc.sbuf_tensor(f"{tag}_{n}", shape, dt))

        def ps(n):
            return ctx.enter_context(nc.psum_tensor(f"{tag}_{n}", [P, 512], F32))

        sem = ctx.enter_context(phase_semaphores(nc, tag))

        wqkv = sb("wqkv", [P, 2, 3 * INNER])
        wo = sb("wo", [P, PAIRS, C])
        w1 = sb("w1", [P, 2 * DI])
        w2 = sb("w2", [P, LF, C])
        ln_g, ln_b = sb("ln_g", [P, 1]), sb("ln_b", [P, 1])
        b1 = sb("b1", [P, 2, LF])
        b2 = sb("b2", [P, C])
        tabs = const["tabs"]
        h_in = sb("h_in", [P, TPS, C])
        xs = sb("xs", [P, NT + 1])
        sq = sb("sq", [P, 2, CH])
        qk = sb("qk", [P, 4, CH])
        swap = sb("swap", [P, 2, CH])
        ss, ssm, rn = [sb(n, [P, 2, HEADS]) for n in ("ss", "ssm", "rn")]
        rq8, nrq8 = sb("rq8", [P, TPS, HEADS]), sb("nrq8", [P, TPS, HEADS])
        minus_half = sb("minus_half", [P, HEADS])
        qT = sb("qT", [P, TPS, PAIRS, P])
        kT = sb("kT", [P, TPS, PAIRS, KEYS])
        v = sb("v", [P, TPS, HEADS, DH + 1])
        mx, nb = sb("mx", [P, HEADS]), sb("nb", [P, HEADS])
        pr = sb("pr", [P, HEADS, KEYS])
        prT = sb("prT", [P, 2, 4, P])
        ppT = sb("ppT", [P, HEADS, WIN])
        rden = sb("rden", [P, 4])
        on = sb("on", [P, HEADS, DH])
        oT = sb("oT", [P, PAIRS, P])
        h_mid = sb("h_mid", [P, TPS, C])
        hb = sb("hb", [P, TPS, C])
        hs = sb("hs", [P, TPS, C])
        fstats = sb("fstats", [P, TPS, 6])
        fmv = sb("fmv", [P, TPS, 2])
        fve, frstd = sb("fve", [P, TPS]), sb("frstd", [P, TPS])
        xn = sb("xn", [P, TPS, C])
        xnT = sb("xnT", [P, NT])
        gate = sb("gate", [P, LF, NT])
        uT = sb("uT", [P, LF, NT])

        QKV = [ps("psQ0"), ps("psQ1")]
        S = [ps("psS0"), ps("psS1")]
        TA, TP = ps("psTA"), ps("psTP")
        O, FB = ps("psO"), ps("psF")

        wqkv_loaded, wo_loaded, wf_loaded = [sem(n) for n in ("wqkv_loaded", "wo_loaded", "wf_loaded")]
        half_ready, set_up = sem("half_ready"), sem("set_up")
        hin_ready, ta_ps, ta_free = sem("hin_ready"), sem("ta_ps"), sem("ta_free")
        qkv_ps, sq_ready, u_ready, w_ready, v_ready, rot_ready = [sem(n) for n in (
            "qkv_ps", "sq_ready", "u_ready", "w_ready", "v_ready", "rot_ready")]
        ss_ready = [sem("ss_ready0"), sem("ss_ready1")]
        ssm_ready, rn_ready, rq_ready, kn_ready = [sem(n) for n in ("ssm_ready", "rn_ready", "rq_ready", "kn_ready")]
        s_ps, mx_ready, nb_ready = sem("s_ps"), sem("mx_ready"), sem("nb_ready")
        s_free = [sem("s_free0"), sem("s_free1")]
        tp_ps, tp_free, ppT_ready = sem("tp_ps"), sem("tp_free"), sem("ppT_ready")
        o_ps, rden_ready, o_free = sem("o_ps"), sem("rden_ready"), sem("o_free")
        f_ps, f_free = sem("f_ps"), sem("f_free")
        hb_ready, hs_ready, fst_ready, fmv_ready, fve_ready, frstd_ready, xn_ready = [sem(n) for n in (
            "hb_ready", "hs_ready", "fst_ready", "fmv_ready", "fve_ready", "frstd_ready", "xn_ready")]
        block = ctx.enter_context(nc.Block())
        ident, down, carry = const["ident"], const["down"], const["carry"]

        V0, O0, F0 = 2, len(O_USE) * TPS, len(F_USE) * NB

        def ta(i, t, part, k):
            return len(TA_USE) * (TPS * i + t) + TA_USE[part, k]

        def tp(i, t, part, k):
            return len(TP_USE) * (TPS * i + t) + TP_USE[part, k]

        def ou(i, t, part, k):
            return len(O_USE) * (TPS * i + t) + O_USE[part, k]

        def fu(i, part, k):
            return len(F_USE) * i + F_USE[part, k]

        def heads8(ap):
            return ap.rearrange("p (h d) -> p h d", d=DH)

        def blocks4(ap):
            return ap.rearrange("p (a x) -> p a x", x=P)

        @block.sync
        def _(sp):
            def load_qkv(l, slot):
                sp.dma_start(wqkv[:, slot, :], w["Wqkv"][l]).then_inc(wqkv_loaded, 16)

            def load_wo(l):
                sp.dma_start(wo[:, :, :], w["Wo"][l].rearrange("(k p) c -> p k c", p=P)).then_inc(wo_loaded, 16)

            def load_ffn(l):
                sp.dma_start(w1[:, :], w["W1"][l]).then_inc(wf_loaded, 16)
                for c, (r0, n) in enumerate(FCH):
                    sp.dma_start(w2[0:n, c, :], w["W2"][l, r0:r0 + n, :]).then_inc(wf_loaded, 16)
                for a in range(2):
                    for c, (r0, n) in enumerate(FCH):
                        sp.dma_start(b1[0:n, a, c:c + 1],
                                     w["b1"][l, a * DI + r0:a * DI + r0 + n].unsqueeze(1)).then_inc(wf_loaded, 16)
                sp.dma_start(b2[:, :], w["b2"][l].partition_broadcast(P)).then_inc(wf_loaded, 16)
                sp.dma_start(ln_g[:, :], w["ln_g"][l].unsqueeze(1)).then_inc(wf_loaded, 16)
                sp.dma_start(ln_b[:, :], w["ln_b"][l].unsqueeze(1)).then_inc(wf_loaded, 16)

            load_qkv(0, 0)
            load_wo(0)
            load_ffn(0)
            with sp.Fori(0, DEPTH - 1) as l:
                sp.wait_ge(qkv_ps, 6 * TILES * l + 1)
                load_qkv(l + 1, (l + 1) % 2)
                sp.wait_ge(o_ps, len(O_USE) * TILES * (l + 1))
                load_wo(l + 1)
                sp.wait_ge(f_free, F0 + len(F_USE) * NB * (l + 1))
                load_ffn(l + 1)

        N_WF = 16 * (1 + LF + 2 * LF + 3)

        @block.gpsimd
        def _(pool):
            nc.gpsimd.memset(minus_half[:], -0.5).then_inc(half_ready, 1)
            pool.wait_ge(half_ready, 1)
            pool.wait_ge(set_up, 1)

            def emit(i, l, x):
                part, t, k = x
                g = TPS * i + t
                if part == "in":
                    pool.wait_ge(f_free, len(F_USE) * (i + 1))
                    pool.wait_ge(o_free, len(O_USE) * (g + 1))
                    pool.nop(nofuse=True)
                    nc.gpsimd.tensor_copy(h_in[:, t, :], h[:, (i % NB) * TPS + t, :]).then_inc(hin_ready, 1)
                elif part == "rotate":
                    pool.wait_ge(w_ready, 4 * g + k + 1)
                    nc.gpsimd.tensor_tensor(qk[:, k, :], qk[:, k, :], swap[:, k % 2, :],
                                            ALU.add).then_inc(rot_ready, 1)
                elif part == "norm":
                    pool.wait_ge(ssm_ready, 2 * g + k + 1)
                    nc.gpsimd.tensor_tensor(rn[:, k, :], ssm[:, k, :], minus_half[:], ALU.pow).then_inc(rn_ready, 1)
                elif part == "shift":
                    pool.wait_ge(o_free, O0 + len(O_USE) * TPS * (i + 1))
                    pool.nop(nofuse=True)
                    nc.gpsimd.tensor_copy(hs[:, :, 0:C // 2], h_mid[:, :, 0:C // 2]).then_inc(hs_ready, 1)
                    pool.wait_ge(wf_loaded, N_WF * (l + 1))
                    nc.gpsimd.tensor_tensor(hb[:], h_mid[:], b2[:].unsqueeze(1).broadcast_to([P, TPS, C]),
                                            ALU.add).then_inc(hb_ready, 1)
                elif part == "stats":
                    pool.wait_ge(fve_ready, i + 1)
                    nc.gpsimd.tensor_tensor(frstd[:], fve[:], minus_half[:, 0:TPS], ALU.pow).then_inc(frstd_ready, 1)

            run_steps(pool, "POOL", emit)

        @block.scalar
        def _(act):
            act.wait_ge(set_up, 1)

            def emit(i, l, x):
                part, t, k = x
                g = TPS * i + t
                if part == "in":
                    act.wait_ge(ta_ps, ta(i, t, part, k) + 1)
                    nc.scalar.activation(xs[0:64, P * t:P * (t + 1)], TA[0:64, 0:P], ACT.Copy)
                    nc.scalar.activation(xs[64:128, P * t + 1:P * (t + 1) + 1], TA[64:128, 0:P],
                                         ACT.Copy).then_inc(ta_free, 1)
                elif part == "qkv" and k < 4:
                    act.wait_ge(qkv_ps, 6 * g + k + 1)
                    act.wait_ge(ss_ready[k % 2], 1 + 2 * g + k // 2)
                    nc.scalar.activation(sq[:, k % 2, :], QKV[k % 2][:, :], ACT.Square).then_inc(sq_ready, 1)
                elif part == "qkv":
                    act.wait_ge(qkv_ps, 6 * g + k + 1)
                    nc.scalar.activation(v[:, t, 8 * (k - 4):8 * (k - 3), 0:DH], heads8(QKV[k % 2][:, :]),
                                         ACT.Copy).then_inc(v_ready, 1)
                elif part == "rot":
                    act.wait_ge(ta_ps, ta(i, t, part, k) + 1)
                    src = blocks4(TA[:, :])
                    if k < 2:
                        last = nc.scalar.activation(qT[:, t, 4 * k:4 * k + 4, :], src, ACT.Copy)
                    else:
                        a = 4 * (k - 2)
                        last = nc.scalar.activation(kT[:, t, a:a + 4, WIN:KEYS], src, ACT.Copy)
                        if t < TPS - 1:
                            last = nc.scalar.activation(kT[:, t + 1, a:a + 4, 0:WIN], src[:, :, P - WIN:P], ACT.Copy)
                    last.then_inc(ta_free, 1)
                elif part == "s":
                    lo = 0 if t else WIN
                    act.wait_ge(nb_ready, PAIRS * g + k + 1)
                    for hh, hd in enumerate(unit_heads(k)):
                        last = nc.scalar.activation(pr[:, hd, lo:KEYS], S[k % 2][:, hh * KEYS + lo:(hh + 1) * KEYS],
                                                    ACT.Exp, bias=nb[:, hd:hd + 1], scale=rq8[:, t, hd:hd + 1])
                    last.then_inc(s_free[k % 2], 1)
                elif part in ("pt", "ot"):
                    act.wait_ge(tp_ps, tp(i, t, part, k) + 1)
                    dst = prT[:, k % 2, :, :] if part == "pt" else oT[:, 4 * k:4 * k + 4, :]
                    nc.scalar.activation(dst, blocks4(TP[:, :]), ACT.Copy).then_inc(tp_free, 1)
                elif part == "xnT":
                    act.wait_ge(f_ps, fu(i, part, k) + 1)
                    act.wait_ge(wf_loaded, N_WF * (l + 1))
                    nc.scalar.activation(xnT[:], FB[:, :], ACT.Identity, bias=ln_b[:, 0:1],
                                         scale=ln_g[:, 0:1]).then_inc(f_free, 1)
                elif part == "gate":
                    n = FCH[k][1]
                    act.wait_ge(f_ps, fu(i, part, k) + 1)
                    nc.scalar.activation(gate[0:n, k, :], FB[0:n, :], ACT.Gelu,
                                         bias=b1[0:n, 1, k:k + 1]).then_inc(f_free, 1)

            run_steps(act, "ACT", emit)

        @block.vector
        def _(dve):
            for sm, n in ((o_free, O0), (f_free, F0), (v_ready, V0), (ta_free, 1), (tp_free, 1), (s_free[0], 1),
                          (s_free[1], 1), (ss_ready[0], 1), (ss_ready[1], 1), (hb_ready, 1)):
                dve.sem_inc(sm, n)
            nc.vector.memset(xs[:, 0:1], 0.0)
            nc.vector.memset(v[:, :, :, DH:DH + 1], 1.0).then_inc(set_up, 1)

            def emit(i, l, x):
                part, t, k = x
                g = TPS * i + t
                if part == "rotate":
                    n = 4 * g + k
                    src = heads8(QKV[k % 2][:, :])
                    cos = tabs[:, l, t, 2 * (k // 2), :].unsqueeze(1).broadcast_to([P, 8, DH])
                    dve.wait_ge(sq_ready, n + 1)
                    nc.vector.tensor_tensor(heads8(qk[:, k, :]), src, cos, ALU.mult)
                    if k >= 2:
                        dve.wait_ge(rot_ready, n - 1)
                    for a, b in ((0, DH // 2), (DH // 2, 0)):
                        sn = tabs[:, l, t, 2 * (k // 2) + 1, a:a + DH // 2].unsqueeze(1).broadcast_to(
                            [P, 8, DH // 2])
                        last = nc.vector.tensor_tensor(heads8(swap[:, k % 2, :])[:, :, a:a + DH // 2],
                                                       src[:, :, b:b + DH // 2], sn, ALU.mult)
                    last.then_inc(w_ready, 1)
                    nc.vector.tensor_reduce(ss[:, k // 2, 8 * (k % 2):8 * (k % 2) + 8], heads8(sq[:, k % 2, :]), AX,
                                            ALU.add).then_inc(ss_ready[k % 2], 1)
                elif part == "norm":
                    for b in range(2):
                        dve.wait_ge(ss_ready[b], 1 + 2 * g + k + 1)
                    nc.vector.tensor_scalar(ssm[:, k, :], ss[:, k, :], 1e-24, None, ALU.max).then_inc(ssm_ready, 1)
                elif part == "scale":
                    dve.wait_ge(rn_ready, 2 * g + k + 1)
                    if k == 0:
                        nc.vector.tensor_scalar(rq8[:, t, :], rn[:, 0, :], QK_SCALE, None, ALU.mult)
                        nc.vector.tensor_scalar(nrq8[:, t, :], rn[:, 0, :], -QK_SCALE, None,
                                                ALU.mult).then_inc(rq_ready, 1)
                    else:
                        for c in range(2, 4):
                            dve.wait_ge(rot_ready, 4 * g + c + 1)
                            r = rn[:, 1, 8 * (c - 2):8 * (c - 1)].unsqueeze(2).broadcast_to([P, 8, DH])
                            nc.vector.tensor_tensor(heads8(qk[:, c, :]), heads8(qk[:, c, :]), r,
                                                    ALU.mult).then_inc(kn_ready, 1)
                elif part == "s":
                    lo = 0 if t else WIN
                    n = PAIRS * g + k
                    dve.wait_ge(s_ps, n + 1)
                    if k == 0:
                        dve.wait_ge(rq_ready, g + 1)
                    sv = S[k % 2][:, 0:2 * KEYS].rearrange("p (h x) -> p h x", x=KEYS)[:, :, lo:KEYS]
                    hs2 = slice(unit_heads(k)[0], unit_heads(k)[1] + 1, 2)
                    nc.vector.tensor_reduce(mx[:, hs2], sv, AX, ALU.max).then_inc(mx_ready, 1)
                    dve.wait_ge(mx_ready, n + 1)
                    nc.vector.tensor_tensor(nb[:, hs2], mx[:, hs2], nrq8[:, t, hs2], ALU.mult).then_inc(nb_ready, 1)
                elif part == "pt" and t:
                    for b in range(2):
                        dve.wait_ge(s_free[b], 1 + PAIRS // 2 * g + k + 1)
                    nc.vector.transpose(ppT[96:128, 4 * k:4 * k + 4, :],
                                        pr[0:WIN, 4 * k:4 * k + 4, 0:WIN]).then_inc(ppT_ready, 1)
                elif part == "pv":
                    n = 4 * g + k
                    ov = O[:, 0:4 * (DH + 1)].rearrange("p (h x) -> p h x", x=DH + 1)
                    dve.wait_ge(o_ps, ou(i, t, part, k) + 1)
                    nc.vector.reciprocal(rden[:, :], ov[:, :, DH]).then_inc(rden_ready, 1)
                    dve.wait_ge(rden_ready, n + 1)
                    nc.vector.tensor_tensor(on[:, 4 * k:4 * k + 4, :], ov[:, :, 0:DH],
                                            rden[:, :].unsqueeze(2).broadcast_to([P, 4, DH]),
                                            ALU.mult).then_inc(o_free, 1)
                elif part == "wo":
                    dve.wait_ge(o_ps, ou(i, t, part, k) + 1)
                    if t == 0:
                        dve.wait_ge(hb_ready, i + 1)
                    nc.vector.tensor_tensor(h_mid[:, t, :], h_in[:, t, :], O[:, 0:C], ALU.add).then_inc(o_free, 1)
                elif part == "shift":
                    dve.wait_ge(f_ps, fu(i, part, k) + 1)
                    nc.vector.tensor_copy(hs[:, :, C // 2:C], FB[:, 0:TPS * C // 2].rearrange(
                        "p (t x) -> p t x", x=C // 2)).then_inc(f_free, 1)
                elif part == "stats":
                    dve.wait_ge(f_free, F0 + fu(i, "shift", 0) + 1)
                    dve.wait_ge(hs_ready, i + 1)
                    for u in range(TPS):
                        nc.vector.bn_stats(fstats[:, u, :], hs[:, u, :]).then_inc(fst_ready, 1)
                    for u in range(TPS):
                        dve.wait_ge(fst_ready, TPS * i + u + 1)
                        dve.nop(nofuse=True)
                        nc.vector.bn_aggr(fmv[:, u, :], fstats[:, u, :]).then_inc(fmv_ready, 1)
                    dve.wait_ge(fmv_ready, TPS * i + TPS)
                    nc.vector.tensor_scalar(fve[:], fmv[:, :, 1], EPS, None, ALU.add).then_inc(fve_ready, 1)
                elif part == "ln":
                    dve.wait_ge(frstd_ready, i + 1)
                    for u in range(TPS):
                        nc.vector.tensor_scalar(xn[:, u, :], hs[:, u, :], fmv[:, u, 0:1], frstd[:, u:u + 1],
                                                ALU.subtract, ALU.mult).then_inc(xn_ready, 1)
                elif part == "lin":
                    n = FCH[k][1]
                    dve.wait_ge(f_ps, fu(i, part, k) + 1)
                    nc.vector.scalar_tensor_tensor(out=uT[0:n, k, :], in0=FB[0:n, :], scalar=b1[0:n, 0, k:k + 1],
                                                   in1=gate[0:n, k, :], op0=ALU.add, op1=ALU.mult
                                                   ).then_inc(f_free, 1)
                elif part == "out":
                    dve.wait_ge(f_ps, fu(i, part, k) + 1)
                    dve.wait_ge(hb_ready, 1 + i + 1)
                    nc.vector.tensor_tensor(h[:, bass.ds((i % NB) * TPS, TPS), :], hb[:],
                                            FB[:, :].rearrange("p (t c) -> p t c", c=C), ALU.add).then_inc(f_free, 1)

            run_steps(dve, "DVE", emit)

        @block.tensor
        def _(pe):
            pe.wait_ge(set_up, 1)

            def emit(i, l, x):
                part, t, k = x
                g = TPS * i + t
                if part == "in":
                    pe.wait_ge(hin_ready, g + 1)
                    pe.wait_ge(ta_free, 1 + ta(i, t, part, k))
                    nc.tensor.transpose(TA[:, 0:P], h_in[:, t, :], ident).then_inc(ta_ps, 1)
                elif part == "qkv":
                    if k == 0:
                        pe.wait_ge(ta_free, 1 + ta(i, t, "in", 0) + 1)
                        if t == 0:
                            pe.wait_ge(wqkv_loaded, 16 * (l + 1))
                    if k < 2:
                        pe.wait_ge(v_ready, V0 - 2 + 2 * g + k + 1)
                    else:
                        pe.wait_ge(w_ready, 4 * g + k - 1)
                    nc.tensor.matmul(QKV[k % 2][:, :], xs[:, P * t:P * (t + 1)],
                                     wqkv[:, l % 2, CH * k:CH * (k + 1)], start=True, stop=True).then_inc(qkv_ps, 1)
                elif part == "rot":
                    if k < 2:
                        pe.wait_ge(rot_ready, 4 * g + k + 1)
                    else:
                        pe.wait_ge(kn_ready, 2 * g + k - 1)
                    pe.wait_ge(ta_free, 1 + ta(i, t, part, k))
                    for a in range(4):
                        last = nc.tensor.transpose(TA[:, P * a:P * (a + 1)], qk[:, k, P * a:P * (a + 1)], ident)
                    last.then_inc(ta_ps, 1)
                elif part == "s":
                    lo = 0 if t else WIN
                    if k == 0:
                        pe.wait_ge(ta_free, 1 + ta(i, t, "rot", 3) + 1)
                    pe.wait_ge(s_free[k % 2], 1 + PAIRS // 2 * g + k // 2)
                    sv = S[k % 2][:, 0:2 * KEYS].rearrange("p (h x) -> p h x", x=KEYS)
                    nc.tensor.matmul(sv[:, :, lo:KEYS], const["ident_bf"], const["mask"][:, :, lo:KEYS],
                                     start=True, stop=False, skip_group_check=True)
                    r = slice(DH * (k % 2), DH * (k % 2) + DH)
                    for hh, hd in enumerate(unit_heads(k)):
                        last = nc.tensor.matmul(sv[:, hh, lo:KEYS], qT[r, t, hd // 2, :], kT[r, t, hd // 2, lo:KEYS],
                                                start=False, stop=True, skip_group_check=True)
                    last.then_inc(s_ps, 1)
                elif part == "pt":
                    pe.wait_ge(tp_free, 1 + tp(i, t, part, k))
                    for b in range(2):
                        pe.wait_ge(s_free[b], 1 + PAIRS // 2 * g + k + 1)
                    for a in range(4):
                        last = nc.tensor.transpose(TP[:, P * a:P * (a + 1)], pr[:, 4 * k + a, WIN:KEYS], ident)
                    last.then_inc(tp_ps, 1)
                elif part == "pv":
                    pe.wait_ge(tp_free, 1 + tp(i, t, "pt", k) + 1)
                    if k == 0:
                        pe.wait_ge(v_ready, V0 + 2 * g + 2)
                    if t:
                        pe.wait_ge(ppT_ready, 4 * (TPS - 1) * i + 4 * (t - 1) + k + 1)
                    pe.wait_ge(o_free, O0 + ou(i, t, part, k))
                    for a in range(4):
                        hd = 4 * k + a
                        last = nc.tensor.matmul(O[:, a * (DH + 1):(a + 1) * (DH + 1)], prT[:, k % 2, a, :],
                                                v[:, t, hd, :], start=True, stop=not t, skip_group_check=True)
                        if t:
                            last = nc.tensor.matmul(O[0:WIN, a * (DH + 1):(a + 1) * (DH + 1)], ppT[96:128, hd, :],
                                                    v[96:128, t - 1, hd, :], start=False, stop=True,
                                                    skip_group_check=True)
                    last.then_inc(o_ps, 1)
                elif part == "ot":
                    pe.wait_ge(tp_free, 1 + tp(i, t, part, k))
                    pe.wait_ge(o_free, O0 + ou(i, t, "pv", 2 * k + 1) + 1)
                    for a in range(4):
                        hd = 8 * k + 2 * a
                        last = nc.tensor.transpose(TP[:, P * a:P * (a + 1)],
                                                   on[:, hd:hd + 2, :].rearrange("p a b -> p (a b)"), ident)
                    last.then_inc(tp_ps, 1)
                elif part == "wo":
                    pe.wait_ge(tp_free, 1 + tp(i, t, "ot", 1) + 1)
                    if t == 0:
                        pe.wait_ge(wo_loaded, 16 * (l + 1))
                    pe.wait_ge(o_free, O0 + ou(i, t, part, k))
                    for c in range(PAIRS):
                        last = nc.tensor.matmul(O[:, 0:C], oT[:, c, :], wo[:, c, :], start=(c == 0),
                                                stop=(c == PAIRS - 1))
                    last.then_inc(o_ps, 1)
                elif part == "shift":
                    pe.wait_ge(o_free, O0 + len(O_USE) * TPS * (i + 1))
                    pe.wait_ge(f_free, F0 + fu(i, part, k))
                    nc.tensor.matmul(FB[:, 0:TPS * 64], down, h_mid[:, :, 64:128], start=True, stop=False,
                                     skip_group_check=True)
                    nc.tensor.matmul(FB[:, 64:TPS * 64], carry, h_mid[:, 0:TPS - 1, 64:128], start=False,
                                     stop=True, skip_group_check=True).then_inc(f_ps, 1)
                elif part == "xnT":
                    pe.wait_ge(xn_ready, TPS * i + TPS)
                    pe.wait_ge(f_free, F0 + fu(i, part, k))
                    for u in range(TPS):
                        last = nc.tensor.transpose(FB[:, P * u:P * (u + 1)], xn[:, u, :], ident)
                    last.then_inc(f_ps, 1)
                elif part in ("gate", "lin"):
                    a = int(part == "gate")
                    r0, n = FCH[k]
                    if a and k == 0:
                        pe.wait_ge(wf_loaded, N_WF * (l + 1))
                    pe.wait_ge(f_free, F0 + fu(i, part, k))
                    nc.tensor.matmul(FB[0:n, :], w1[:, a * DI + r0:a * DI + r0 + n], xnT[:], start=True,
                                     stop=True).then_inc(f_ps, 1)
                elif part == "out":
                    pe.wait_ge(f_free, F0 + fu(i, part, k))
                    for u in range(TPS):
                        for c, (_, n) in enumerate(FCH):
                            last = nc.tensor.matmul(FB[:, C * u:C * (u + 1)], uT[0:n, c, P * u:P * (u + 1)],
                                                    w2[0:n, c, :], start=(c == 0), stop=(c == LF - 1))
                    last.then_inc(f_ps, 1)

            run_steps(pe, "PE", emit)


def alibi_phase(nc, x, h, const, w):
    units = TPS * H2
    GR = H2 // 4
    TABW = 2 * NT - P
    slopes = alibi_slopes()
    LAG_T, LAG_PV, LAG_ON, LAG_WP = 2, 3, 6, 8

    with ExitStack() as ctx:
        def sb(n, shape, dt=F32):
            return ctx.enter_context(nc.sbuf_tensor(f"al_{n}", shape, dt))

        def ps(n):
            return ctx.enter_context(nc.psum_tensor(f"al_{n}", [P, 512], F32))

        sem = ctx.enter_context(phase_semaphores(nc, "al"))

        wraw = sb("wraw", [P, 3 * C])
        wpad = sb("wpad", [P, 2, GR, 4, 32])
        bpad = sb("bpad", [P, 2, GR])
        bqs = sb("bqs", [P, GR])
        bv, bo = sb("bv", [P, C]), sb("bo", [P, C])
        wp = sb("wp", [P, C])
        dist = sb("dist", [P, TABW])
        tab = sb("tab", [P, H2, TABW])
        z = sb("z", [P, TPS, C])
        zT = sb("zT", [P, NT])
        qkT = sb("qkT", [P, 2 * GR, NT])
        v = sb("v", [P, TPS, H2, D2 + 1])
        sc = sb("sc", [P, 2, NT])
        nm = sb("nm", [P, units])
        pr = sb("pr", [P, 2, NT])
        prT = sb("prT", [P, 2, NT])
        rden = sb("rden", [P, H2])
        on = sb("on", [P, H2, D2])
        onT = sb("onT", [P, P])
        S = [ps("psS0"), ps("psS1")]
        T = [ps("psT0"), ps("psT1")]
        A = [ps("psA0"), ps("psA1")]
        M, N = ps("psM"), ps("psN")

        (loaded, zeroed, pad_ready, tab_ready, ones_ready, xb_ready, z_ready, zT_ps, zT_ready, v_ps, v_ready,
         s_ps, sc_ready, exp_ready, pT_ps, pv_ps, rden_ready, on_ready, onT_ps, onT_ready, y_ps, x_done,
         v_zero) = [sem(n) for n in (
             "loaded", "zeroed", "pad_ready", "tab_ready", "ones_ready", "xb_ready", "z_ready", "zT_ps",
             "zT_ready", "v_ps", "v_ready", "s_ps", "sc_ready", "exp_ready", "pT_ps", "pv_ps", "rden_ready",
             "on_ready", "onT_ps", "onT_ready", "y_ps", "x_done", "v_zero")]
        qk_ps = sem("qk_ps")
        qk_ready = [sem("qk_ready0"), sem("qk_ready1")]
        pT_ready = [sem("pT_ready0"), sem("pT_ready1")]
        block = ctx.enter_context(nc.Block())
        ident = const["ident"]
        N_LOAD = 16 * (5 + 8)

        @block.sync
        def _(sp):
            sp.dma_start(wraw[:], w["W_qkv"][:, :]).then_inc(loaded, 16)
            sp.dma_start(wp[:], w["W_proj"][:, :]).then_inc(loaded, 16)
            sp.dma_start(bv[:], w["b_qkv"][2 * C:3 * C].partition_broadcast(P)).then_inc(loaded, 16)
            sp.dma_start(bo[:], w["b_proj"][:].partition_broadcast(P)).then_inc(loaded, 16)
            sp.dma_start(dist[:], w["dist"][:, :]).then_inc(loaded, 16)
            sp.wait_ge(zeroed, 1)
            for n in range(2):
                src = w["b_qkv"][n * C:(n + 1) * C].rearrange("(c j d) -> j d c", j=4, d=D2)
                for j in range(4):
                    sp.dma_start(bpad[32 * j:32 * j + D2, n, :], src[j], allow_slow_non_contiguous=True).then_inc(loaded, 16)

        @block.gpsimd
        def _(pool):
            pool.wait_ge(zeroed, 1)
            pool.wait_ge(loaded, N_LOAD)
            nc.gpsimd.tensor_tensor(x[:], x[:], bo[:].unsqueeze(1).broadcast_to([P, TILES, C]),
                                    ALU.add).then_inc(xb_ready, 1)
            with pool.Fori(0, NB) as b:
                pool.wait_ge(zT_ps, CREDIT + b)
                nc.gpsimd.tensor_copy(z[:], h[:, bass.ds(b * TPS, TPS), :]).then_inc(z_ready, 1)

        @block.scalar
        def _(act):
            act.wait_ge(pad_ready, 1)
            with act.Fori(0, NB) as b:
                act.wait_ge(zT_ps, CREDIT + b + 1)
                nc.scalar.activation(zT[:], M[:, :], ACT.Copy).then_inc(zT_ready, 1)
                for c in range(2 * GR):
                    act.wait_ge(qk_ps, 2 * GR * b + c + 1)
                    if c < GR:
                        nc.scalar.activation(qkT[:, c, :], A[c % 2][:, :], ACT.Identity, bias=bqs[:, c:c + 1],
                                             scale=float(D2) ** -0.5).then_inc(qk_ready[c % 2], 1)
                    else:
                        nc.scalar.activation(qkT[:, c, :], A[c % 2][:, :], ACT.Identity,
                                             bias=bpad[:, 1, c - GR:c - GR + 1]).then_inc(qk_ready[c % 2], 1)
                for k in range(units + LAG_WP + 1):
                    if k < units:
                        act.wait_ge(sc_ready, CREDIT + units * b + k + 1)
                        if k >= 2:
                            act.wait_ge(pT_ps, units * b + k - 1)
                        nc.scalar.activation(pr[:, k % 2, :], sc[:, k % 2, :], ACT.Exp, bias=nm[:, k:k + 1],
                                             scale=-1.0).then_inc(exp_ready, 1)
                    u = k - LAG_T
                    if 0 <= u < units and u % 2 == 0:
                        act.wait_ge(pT_ps, units * b + u + 1)
                        nc.scalar.activation(prT[:, 0, :], T[0][:, :], ACT.Copy).then_inc(pT_ready[0], 1)
                    if k >= H2 + LAG_ON and (k - LAG_ON) % H2 == 0:
                        qt = (k - LAG_ON) // H2 - 1
                        act.wait_ge(onT_ps, TPS * b + qt + 1)
                        nc.scalar.activation(onT[:], M[:, 0:P], ACT.Copy).then_inc(onT_ready, 1)

        @block.vector
        def _(dve):
            for sm in (zT_ps, exp_ready, onT_ready, on_ready, x_done, sc_ready, *qk_ready, *pT_ready):
                dve.sem_inc(sm, CREDIT)
            nc.vector.memset(wpad[:], 0.0)
            nc.vector.memset(bpad[:], 0.0)
            nc.vector.memset(v[:, :, :, D2:D2 + 1], 1.0).then_inc(zeroed, 1)
            dve.wait_ge(zeroed, 1)
            dve.wait_ge(loaded, N_LOAD)
            for n in range(2):
                nc.vector.tensor_copy(wpad[:, n, :, :, 0:D2],
                                      wraw[:, n * C:(n + 1) * C].rearrange("p (c j d) -> p c j d", j=4, d=D2))
            nc.vector.tensor_scalar(bqs[:], bpad[:, 0, :], float(D2) ** -0.5, None, ALU.mult).then_inc(pad_ready, 1)
            for hd in range(H2):
                nc.vector.tensor_scalar(tab[:, hd, :], dist[:], slopes[hd], None, ALU.mult).then_inc(tab_ready, 1)
            dve.wait_ge(tab_ready, H2)
            with dve.Fori(0, NB) as b:
                dve.wait_ge(v_ps, b + 1)
                nc.vector.tensor_tensor(v[:, :, :, 0:D2], N[:, :].rearrange("p (t h d) -> p t h d", h=H2, d=D2),
                                        bv[:].rearrange("p (h d) -> p h d", d=D2).unsqueeze(1).broadcast_to(
                                            [P, TPS, H2, D2]), ALU.add).then_inc(v_ready, 1)
                for k in range(units + LAG_WP + 1):
                    if k < units:
                        qt, hd = k // H2, k % H2
                        dve.wait_ge(s_ps, units * b + k + 1)
                        dve.wait_ge(exp_ready, CREDIT + units * b + k - 1) if k >= 2 else dve.wait_ge(exp_ready, CREDIT + units * b)
                        off = NT - P - P * qt
                        dve.nop(nofuse=True)
                        nc.vector.tensor_tensor_reduce(sc[:, k % 2, :], S[k % 2][:, :], tab[:, hd, off:off + NT],
                                                       -1.0, 0.0, ALU.add, ALU.min, nm[:, k:k + 1]
                                                       ).then_inc(sc_ready, 1)
                    u = k - LAG_T
                    if 0 <= u < units and u % 2:
                        dve.wait_ge(pT_ps, units * b + u + 1)
                        nc.vector.tensor_copy(prT[:, 1, :], T[1][:, :]).then_inc(pT_ready[1], 1)
                    if k >= H2 + LAG_PV and (k - LAG_PV) % H2 == 0:
                        qt = (k - LAG_PV) // H2 - 1
                        ov = A[qt % 2][:, 0:H2 * (D2 + 1)].rearrange("p (h x) -> p h x", x=D2 + 1)
                        dve.wait_ge(pv_ps, units * b + H2 * qt + H2)
                        nc.vector.reciprocal(rden[:], ov[:, :, D2]).then_inc(rden_ready, 1)
                        dve.wait_ge(rden_ready, TPS * b + qt + 1)
                        nc.vector.tensor_tensor(on[:], ov[:, :, 0:D2], rden[:].unsqueeze(2).broadcast_to([P, H2, D2]),
                                                ALU.mult).then_inc(on_ready, 1)
                    if k >= H2 + LAG_WP and (k - LAG_WP) % H2 == 0:
                        qt = (k - LAG_WP) // H2 - 1
                        dve.wait_ge(y_ps, TPS * b + qt + 1)
                        dve.wait_ge(xb_ready, 1)
                        nc.vector.tensor_tensor(x[:, b * TPS + qt, :], x[:, b * TPS + qt, :], N[:, 0:C],
                                                ALU.add).then_inc(x_done, 1)

        @block.tensor
        def _(pe):
            pe.wait_ge(pad_ready, 1)
            pe.wait_ge(zeroed, 1)
            pe.wait_ge(loaded, N_LOAD)
            with pe.Fori(0, NB) as b:
                pe.wait_ge(z_ready, b + 1)
                pe.wait_ge(onT_ready, CREDIT + TPS * b)
                for t in range(TPS):
                    last = nc.tensor.transpose(M[:, P * t:P * (t + 1)], z[:, t, :], ident)
                last.then_inc(zT_ps, 1)
                pe.wait_ge(zT_ready, b + 1)
                pe.wait_ge(on_ready, CREDIT + TPS * b)
                for c in range(2 * GR):
                    pe.wait_ge(qk_ready[c % 2], CREDIT + GR * b + c // 2)
                    nc.tensor.matmul(A[c % 2][:, :], wpad[:, c // GR, c % GR, :, :].rearrange("p j d -> p (j d)"),
                                     zT[:], start=True, stop=True).then_inc(qk_ps, 1)
                pe.wait_ge(x_done, CREDIT + TPS * b)
                for t in range(TPS):
                    last = nc.tensor.matmul(N[:, C * t:C * (t + 1)], zT[:, P * t:P * (t + 1)], wraw[:, 2 * C:3 * C],
                                            start=True, stop=True)
                last.then_inc(v_ps, 1)
                for q in qk_ready:
                    pe.wait_ge(q, CREDIT + GR * b + GR)
                pe.wait_ge(v_ready, b + 1)
                for k in range(units + LAG_WP + 1):
                    if k < units:
                        qt, hd = k // H2, k % H2
                        c, j = hd // 4, 32 * (hd % 4)
                        if k >= 2:
                            pe.wait_ge(sc_ready, CREDIT + units * b + k - 1)
                        else:
                            pe.wait_ge(sc_ready, CREDIT + units * b)
                        nc.tensor.matmul(S[k % 2][:, :], qkT[j:j + D2, c, P * qt:P * (qt + 1)],
                                         qkT[j:j + D2, GR + c, :], start=True, stop=True).then_inc(s_ps, 1)
                    u = k - LAG_T
                    if 0 <= u < units:
                        pe.wait_ge(exp_ready, CREDIT + units * b + u + 1)
                        pe.wait_ge(pT_ready[u % 2], CREDIT + units // 2 * b + u // 2)
                        for a in range(TPS):
                            last = nc.tensor.transpose(T[u % 2][:, P * a:P * (a + 1)],
                                                       pr[:, u % 2, P * a:P * (a + 1)], ident)
                        last.then_inc(pT_ps, 1)
                    u = k - LAG_PV
                    if 0 <= u < units:
                        qt, hd = u // H2, u % H2
                        pe.wait_ge(pT_ready[u % 2], CREDIT + units // 2 * b + u // 2 + 1)
                        if hd == 0 and qt >= 2:
                            pe.wait_ge(on_ready, CREDIT + TPS * b + qt - 1)
                        for a in range(TPS):
                            last = nc.tensor.matmul(A[qt % 2][:, hd * (D2 + 1):(hd + 1) * (D2 + 1)],
                                                    prT[:, u % 2, P * a:P * (a + 1)], v[:, a, hd, :],
                                                    start=(a == 0), stop=(a == TPS - 1), skip_group_check=True)
                        last.then_inc(pv_ps, 1)
                    if k >= H2 + LAG_ON and (k - LAG_ON) % H2 == 0:
                        qt = (k - LAG_ON) // H2 - 1
                        pe.wait_ge(on_ready, CREDIT + TPS * b + qt + 1)
                        pe.wait_ge(onT_ready, CREDIT + TPS * b + qt)
                        nc.tensor.transpose(M[:, 0:P], on[:].rearrange("p h d -> p (h d)"), ident).then_inc(onT_ps, 1)
                    if k >= H2 + LAG_WP and (k - LAG_WP) % H2 == 0:
                        qt = (k - LAG_WP) // H2 - 1
                        pe.wait_ge(onT_ready, CREDIT + TPS * b + qt + 1)
                        pe.wait_ge(x_done, CREDIT + TPS * b + qt)
                        nc.tensor.matmul(N[:, 0:C], onT[:], wp[:], start=True, stop=True).then_inc(y_ps, 1)


def rotary_tables(nc, tabs, eye3, ident_bf, mask, c_eye, c_mask, c_rot, q_scale, k_scale):
    with ExitStack() as ctx:
        mask_f = ctx.enter_context(nc.sbuf_tensor("mask_f", [P, 2, KEYS], F32))
        rotary = ctx.enter_context(nc.sbuf_tensor("rotary", [P, TPS, 4, DH], F32))
        gain = ctx.enter_context(nc.sbuf_tensor("gain", [P, 2, DEPTH, DH], F32))
        sem = ctx.enter_context(phase_semaphores(nc, "c"))
        loaded, made = sem("loaded"), sem("made")
        block = ctx.enter_context(nc.Block())

        @block.sync
        def _(sp):
            sp.dma_start(rotary[:], c_rot).then_inc(loaded, 16)
            for n, g in enumerate((q_scale, k_scale)):
                sp.dma_start(gain[:, n, :, :].rearrange("p l d -> p (l d)"),
                             g.rearrange("l d -> (l d)").partition_broadcast(P)).then_inc(loaded, 16)
            sp.dma_start(eye3[:], c_eye).then_inc(loaded, 16)
            sp.dma_start(mask_f[:], c_mask).then_inc(loaded, 16)

        def tables(eng, layers):
            half = DH // 2
            for l in layers:
                for n in range(2):
                    for a, b, m in ((0, DH, 0), (0, half, 1), (half, DH, 1)):
                        src = (a + half) % DH if m else a
                        g = gain[:, n, l, src:src + b - a].unsqueeze(1).broadcast_to([P, TPS, b - a])
                        last = eng.tensor_tensor(tabs[:, l, :, 2 * n + m, a:b], rotary[:, :, 2 * n + m, a:b], g,
                                                 ALU.mult)
            return last

        @block.gpsimd
        def _(pool):
            pool.wait_ge(loaded, 80)
            tables(nc.gpsimd, range(4, DEPTH)).then_inc(made, 1)

        @block.vector
        def _(dve):
            dve.wait_ge(loaded, 80)
            nc.vector.tensor_copy(ident_bf[:], eye3[:, 0:P])
            nc.vector.tensor_copy(mask[:], mask_f[:])
            tables(nc.vector, range(4)).then_inc(made, 1)


def build(nc, ins, out):
    with ExitStack() as ctx:
        def sb(n, shape, dt=F32):
            return ctx.enter_context(nc.sbuf_tensor(n, shape, dt))

        def constant(name, array, dt=F32):
            return nc.inline_tensor(np.ascontiguousarray(array), name).ap()

        eye3 = sb("eye3", [P, 3 * P])
        ident_bf = sb("ident_bf", [P, P], BF16)
        mask = sb("mask", [P, 2, KEYS], BF16)
        tabs = sb("tabs", [P, DEPTH, TPS, 4, DH])
        x = sb("x", [P, TILES, C])
        h = sb("h", [P, TILES, C])
        c_eye = constant("c_eye3", shift_matrices())
        c_mask = constant("c_mask", window_mask().astype(np.float32))
        c_rot = constant("c_rotary", rotary_constants())
        d = np.arange(2 * NT - P)[None, :] - (NT - P) - np.arange(P)[:, None]
        c_dist = constant("c_dist", np.minimum(d, 0).astype(np.float32))
        const = {"ident": eye3[:, 0:P], "down": eye3[:, P:2 * P], "carry": eye3[:, 2 * P:3 * P],
                 "ident_bf": ident_bf[:], "mask": mask[:], "tabs": tabs[:]}
        rotary_tables(nc, tabs, eye3, ident_bf, mask, c_eye, c_mask, c_rot, ins["L0_ffn_q_scale"],
                      ins["L0_ffn_k_scale"])
        f_w = {n: ins["L0_ffn_" + n] for n in ("Wqkv", "q_scale", "k_scale", "Wo", "ln_g", "ln_b", "W1", "b1",
                                               "W2", "b2")}
        a_w = {n: ins["L0_attn_" + n] for n in ("W_qkv", "b_qkv", "W_proj", "b_proj")}
        a_w["dist"] = c_dist
        layer_norm_phase(nc, "n1", x, h, ins["L0_attn_x"], None, None)
        macaron_phase(nc, "f1", h, const, f_w)
        layer_norm_phase(nc, "n2", x, h, None, 0.5, None)
        alibi_phase(nc, x, h, const, a_w)
        layer_norm_phase(nc, "n3", x, h, None, None, None)
        macaron_phase(nc, "f2", h, const, f_w)
        layer_norm_phase(nc, "end", x, h, None, 0.5, out)


_INS = ["L0_attn_x", "L0_attn_W_qkv", "L0_attn_b_qkv", "L0_attn_W_proj", "L0_attn_b_proj", "L0_ffn_Wqkv",
        "L0_ffn_q_scale", "L0_ffn_k_scale", "L0_ffn_Wo", "L0_ffn_ln_g", "L0_ffn_ln_b", "L0_ffn_W1", "L0_ffn_b1",
        "L0_ffn_W2", "L0_ffn_b2"]


def kernel(**inputs):
    import concourse.bacc as bacc
    from concourse.bass_utils import run_bass_kernel_spmd

    nc = bacc.Bacc("TRN2", target_bir_lowering=False, num_devices=1)
    arrays, ins = {}, {}
    for name in _INS:
        a = np.ascontiguousarray(inputs[name])
        arrays[f"in_{name}"] = a
        ins[name] = nc.dram_tensor(f"in_{name}", a.shape, mybir.dt.from_np(a.dtype), kind="ExternalInput").ap()
    out = nc.dram_tensor("out_x", (NB, NT, C), F32, kind="ExternalOutput").ap()
    build(nc, ins, out)
    r = run_bass_kernel_spmd(nc, [arrays], core_ids=[0])
    return r.results[0]["out_x"]
```

```python
from contextlib import ExitStack, contextmanager

import numpy as np
import concourse.bass as bass
from concourse import mybir

F32 = mybir.dt.float32
F32R = mybir.dt.float32r
ALU = mybir.AluOpType
ACT = mybir.ActivationFunctionType
AX = mybir.AxisListType.X

P = 128
NB, NT, C = 4, 512, 128
TPS = NT // P
TILES = NB * TPS
DEPTH, HEADS, DH, WIN = 6, 16, 64, 32
INNER = HEADS * DH
PAIRS = HEADS // 2
KEYS = P + WIN
CH = 512
DI = C * 4 * 2 // 3
FCH = [(0, 128), (128, 128), (256, DI - 256)]
QK_SCALE = 8.0
EPS = 1e-5
MASKED = -1e30
HUGE = 3e38
H2, D2 = 16, 8
STEPS = DEPTH * NB
CREDIT = 1


def rotary_constants():
    f = np.float32
    half = np.arange(0, DH, 2, dtype=f)
    inv_freq = (f(1.0) / np.power(f(10000.0), half / f(DH))).astype(f)
    t = np.arange(NT, dtype=f)
    freqs = t[:, None] * inv_freq[None, :]
    freqs = np.concatenate([freqs, freqs], -1)
    base = (half + f(0.4 * DH)) / f(1.4 * DH)
    power = (t - f(NT // 2)) / f(WIN // 2)
    scale = np.power(base[None, :], power[:, None]).astype(f)
    scale = np.concatenate([scale, scale], -1)
    cos, sin = np.cos(freqs).astype(f), np.sin(freqs).astype(f)
    sin[:, :DH // 2] *= f(-1.0)
    inv = (f(1.0) / scale).astype(f)
    tabs = np.stack([cos * scale, sin * scale, cos * inv, sin * inv], 1)
    return np.ascontiguousarray(tabs.reshape(TPS, P, 4, DH).transpose(1, 0, 2, 3)).astype(f)


def window_mask():
    d = np.arange(KEYS)[None, :] - np.arange(P)[:, None]
    return np.where((d >= 0) & (d <= WIN), 0.0, MASKED)


def alibi_slopes():
    start = 2 ** (-2 ** (-(np.log2(H2) - 3)))
    return [float(start * start ** i) for i in range(H2)]


def shift_matrices():
    down, carry = np.eye(P, k=1, dtype=np.float32), np.zeros((P, P), np.float32)
    carry[P - 1, 0] = 1.0
    return np.concatenate([np.eye(P, dtype=np.float32), down, carry], 1)


@contextmanager
def phase_semaphores(nc, tag):
    made = []

    def sem(name):
        made.append(nc.alloc_semaphore(f"{tag}_{name}"))
        return made[-1]

    yield sem
    nc.clear_and_free_semaphores(made)
    nc.all_engine_barrier()


SLOTS = 8 * TPS
TILE_PARTS = {
    ("in", 0): {"PE": 6.62, "ACT": 6.75, "DVE": 6.48, "POOL": 0.08},
    ("qkv", 0): {"PE": 6.84, "ACT": 7.63},
    ("qkv", 1): {"PE": 8.00, "ACT": 8.68},
    ("qkv", 2): {"PE": 9.90, "ACT": 9.95},
    ("qkv", 3): {"PE": 10.66, "ACT": 10.46},
    ("qkv", 4): {"PE": 12.63, "ACT": 11.89},
    ("qkv", 5): {"PE": 13.46, "ACT": 14.65},
    ("rotate", 0): {"DVE": 7.87, "POOL": 9.39},
    ("rotate", 1): {"DVE": 9.35, "POOL": 10.23},
    ("rotate", 2): {"DVE": 9.66, "POOL": 12.06},
    ("rotate", 3): {"DVE": 9.71, "POOL": 12.16},
    ("norm", 0): {"DVE": 9.51, "POOL": 11.60},
    ("norm", 1): {"DVE": 10.15, "POOL": 12.11},
    ("scale", 0): {"DVE": 13.49},
    ("scale", 1): {"DVE": 13.21},
    ("rot", 0): {"PE": 11.94, "ACT": 11.55},
    ("rot", 1): {"PE": 12.80, "ACT": 12.41},
    ("rot", 2): {"PE": 13.54, "ACT": 13.78},
    ("rot", 3): {"PE": 14.04, "ACT": 14.25},
    ("s", 0): {"PE": 14.67, "ACT": 16.52, "DVE": 14.53},
    ("s", 1): {"PE": 14.76, "ACT": 16.57, "DVE": 14.98},
    ("s", 2): {"PE": 15.06, "ACT": 16.88, "DVE": 15.30},
    ("s", 3): {"PE": 18.03, "ACT": 19.22, "DVE": 17.38},
    ("s", 4): {"PE": 18.18, "ACT": 21.41, "DVE": 19.06},
    ("s", 5): {"PE": 20.65, "ACT": 21.14, "DVE": 19.30},
    ("s", 6): {"PE": 20.88, "ACT": 22.12, "DVE": 20.51},
    ("s", 7): {"PE": 21.27, "ACT": 22.88, "DVE": 22.09},
    ("nb", 0): {"DVE": 15.08},
    ("nb", 1): {"DVE": 15.14},
    ("nb", 2): {"DVE": 16.03},
    ("nb", 3): {"DVE": 17.52},
    ("nb", 4): {"DVE": 19.42},
    ("nb", 5): {"DVE": 19.57},
    ("nb", 6): {"DVE": 20.73},
    ("nb", 7): {"DVE": 22.14},
    ("weigh", 0): {"DVE": 17.24, "POOL": 17.79},
    ("weigh", 1): {"DVE": 20.10, "POOL": 20.49},
    ("weigh", 2): {"DVE": 21.56, "POOL": 22.50},
    ("weigh", 3): {"DVE": 23.59, "POOL": 24.56},
    ("pt", 0): {"PE": 19.11, "ACT": 20.38, "DVE": 20.82},
    ("pt", 1): {"PE": 22.38, "ACT": 23.56, "DVE": 22.88},
    ("pt", 2): {"PE": 24.46, "ACT": 25.35, "DVE": 23.13},
    ("pt", 3): {"PE": 26.65, "ACT": 26.36, "DVE": 24.99},
    ("pv", 0): {"PE": 21.99},
    ("pv", 1): {"PE": 24.34, "ACT": 25.49},
    ("pv", 2): {"PE": 26.89},
    ("pv", 3): {"PE": 27.64, "DVE": 27.17},
    ("wo", 0): {"PE": 29.10, "DVE": 28.85},
}
FFN_PARTS = {
    ("split", 0): {"POOL": 14.94},
    ("shift", 0): {"PE": 53.85, "DVE": 53.75, "POOL": 53.48},
    ("stats", 0): {"DVE": 54.17, "POOL": 54.67},
    ("ln", 0): {"DVE": 56.39},
    ("xnT", 0): {"PE": 58.27, "ACT": 58.36},
    ("gate", 0): {"PE": 59.41, "ACT": 59.39},
    ("gate", 1): {"PE": 60.72, "ACT": 60.28},
    ("gate", 2): {"PE": 61.10, "ACT": 60.99},
    ("lin", 0): {"PE": 61.38, "DVE": 61.45},
    ("lin", 1): {"PE": 61.68, "DVE": 61.59},
    ("lin", 2): {"PE": 62.31, "DVE": 62.34},
    ("out", 0): {"PE": 63.40, "DVE": 63.96},
}
TA_USE = {("in", 0): 0, **{("rot", k): 1 + k for k in range(4)}}
TP_USE = {("pt", k): k for k in range(4)}
O_USE = {("pv", 1): 0, ("pv", 3): 1, ("wo", 0): 2}
F_USE = {("shift", 0): 0, ("xnT", 0): 1, **{("gate", c): 2 + c for c in range(3)},
         **{("lin", c): 5 + c for c in range(3)}, ("out", 0): 8}


def engine_schedule(engine):
    at = [(slots[engine] + 8 * t, (n, t, k)) for (n, k), slots in TILE_PARTS.items() if engine in slots
          for t in range(TPS)]
    at += [(slots[engine], (n, 0, k)) for (n, k), slots in FFN_PARTS.items() if engine in slots]
    assert all(0 <= y < 2 * SLOTS for y, _ in at)
    return [(part, int(y // SLOTS)) for y, part in sorted(at, key=lambda z: (z[0] % SLOTS, z[1]))]


def run_steps(eng, engine, emit):
    parts = engine_schedule(engine)
    for part, lag in parts:
        if lag == 0:
            emit(0, 0, part)
    with eng.Fori(1, STEPS) as j:
        layer = [eng.snap(j // NB), eng.snap((j - 1) // NB)]
        for part, lag in parts:
            emit(j - lag, layer[lag], part)
    for part, lag in parts:
        if lag == 1:
            emit(STEPS - 1, DEPTH - 1, part)


def unit_heads(k):
    return [4 * (k // 2) + k % 2, 4 * (k // 2) + k % 2 + 2]


def layer_norm_parts(sb, sem, stats):
    ln = {"stats": stats, "mv": sb("ln_mv", [P, TILES, 2])}
    ln.update({n: sb("ln_" + n, [P, TILES]) for n in ("ve", "mh", "rstd")})
    ln.update({n: sem("ln_" + n) for n in ("mh_ready", "stats_ready", "mv_ready", "ve_ready", "rstd_ready", "h_ready")})
    return ln


def layer_norm_vector(nc, dve, ln, x, h):
    stats, mv, ve, rstd = ln["stats"], ln["mv"], ln["ve"], ln["rstd"]
    nc.vector.memset(ln["mh"][:], -0.5).then_inc(ln["mh_ready"], 1)
    for n in range(TILES):
        nc.vector.bn_stats(stats[:, n, :], x[:, n, :]).then_inc(ln["stats_ready"], 1)
    for n in range(TILES):
        dve.wait_ge(ln["stats_ready"], n + 1)
        nc.vector.bn_aggr(mv[:, n, :], stats[:, n, :]).then_inc(ln["mv_ready"], 1)
    dve.wait_ge(ln["mv_ready"], TILES)
    nc.vector.tensor_scalar(ve[:], mv[:, :, 1], EPS, None, ALU.add).then_inc(ln["ve_ready"], 1)
    dve.wait_ge(ln["rstd_ready"], 1)
    for n in range(TILES):
        nc.vector.tensor_scalar(h[:, n, :], x[:, n, :], mv[:, n, 0:1], rstd[:, n:n + 1],
                                ALU.subtract, ALU.mult).then_inc(ln["h_ready"], 1)


def layer_norm_pool(nc, pool, ln):
    pool.wait_ge(ln["mh_ready"], 1)
    pool.wait_ge(ln["ve_ready"], 1)
    nc.gpsimd.tensor_tensor(ln["rstd"][:], ln["ve"][:], ln["mh"][:], ALU.pow).then_inc(ln["rstd_ready"], 1)


def output_phase(nc, x, h, out):
    with ExitStack() as ctx:
        sem = ctx.enter_context(phase_semaphores(nc, "end"))
        x_ready, stored = sem("x_ready"), sem("stored")
        block = ctx.enter_context(nc.Block())

        @block.vector
        def _(dve):
            for b in range(NB):
                sl = slice(b * TPS, (b + 1) * TPS)
                nc.vector.scalar_tensor_tensor(out=x[:, sl, :], in0=h[:, sl, :], scalar=0.5, in1=x[:, sl, :],
                                               op0=ALU.mult, op1=ALU.add).then_inc(x_ready, 1)

        @block.sync
        def _(sp):
            for b in range(NB):
                sp.wait_ge(x_ready, b + 1)
                sp.dma_start(out[b].rearrange("(t p) c -> p t c", p=P),
                             x[:, b * TPS:(b + 1) * TPS, :]).then_inc(stored, 16)
            sp.wait_ge(stored, 16 * NB)


def macaron_phase(nc, tag, x, h, const, w):
    LF = len(FCH)
    WSTAGE = 3 * INNER // NB
    with ExitStack() as ctx:
        def sb(n, shape, dt=F32):
            return ctx.enter_context(nc.sbuf_tensor(f"{tag}_{n}", shape, dt))

        def ps(n):
            return ctx.enter_context(nc.psum_tensor(f"{tag}_{n}", [P, 512], F32))

        sem = ctx.enter_context(phase_semaphores(nc, tag))

        wstage = sb("wstage", [P, WSTAGE])
        w_high = sb("w_high", [P, 2, 3 * INNER], F32R)
        w_low = sb("w_low", [P, 2, 3 * INNER], F32R)
        wo = sb("wo", [P, PAIRS, C])
        w1 = sb("w1", [P, 2 * DI])
        w2 = sb("w2", [P, LF, C])
        ln_g, ln_b = sb("ln_g", [P, 1]), sb("ln_b", [P, 1])
        b1 = sb("b1", [P, 2, LF])
        b2 = sb("b2", [P, C])
        tabs = const["tabs"]
        h_in = sb("h_in", [P, TPS, C])
        xs_high = sb("xs_high", [P, NT + 1], F32R)
        xs_low = sb("xs_low", [P, NT + 1], F32R)
        sq = sb("sq", [P, 2, CH])
        qk = sb("qk", [P, 4, CH])
        swap = sb("swap", [P, 2, CH])
        ss, ssm, rn = [sb(n, [P, 2, HEADS]) for n in ("ss", "ssm", "rn")]
        rq8, nrq8 = sb("rq8", [P, TPS, HEADS]), sb("nrq8", [P, TPS, HEADS])
        minus_half = sb("minus_half", [P, HEADS])
        qT = sb("qT", [P, 2, PAIRS, P])
        kT = sb("kT", [P, TPS, PAIRS, KEYS])
        v = sb("v", [P, TPS, HEADS, DH])
        mn, nb = sb("mn", [P, HEADS]), sb("nb", [P, HEADS])
        pr = sb("pr", [P, HEADS, KEYS])
        ln = layer_norm_parts(sb, sem, pr[:, 0, 0:TILES * 6].rearrange("p (n s) -> p n s", s=6))
        prT = sb("prT", [P, 2, 4, P])
        ppT = sb("ppT", [P, HEADS, WIN])
        row_sum, rden = sb("row_sum", [P, HEADS]), sb("rden", [P, HEADS])
        oT = sb("oT", [P, PAIRS, P])
        h_mid = sb("h_mid", [P, TPS, C])
        hb = sb("hb", [P, TPS, C])
        hs = sb("hs", [P, TPS, C])
        fstats = sb("fstats", [P, TPS, 6])
        fmv = sb("fmv", [P, TPS, 2])
        fve, frstd = sb("fve", [P, TPS]), sb("frstd", [P, TPS])
        xnT = sb("xnT", [P, NT])
        gate = sb("gate", [P, LF, NT])

        QKV = [ps("psQ0"), ps("psQ1")]
        S = [ps("psS0"), ps("psS1")]
        TA, TP = ps("psTA"), ps("psTP")
        O, FB = ps("psO"), ps("psF")

        w_staged, wo_loaded, wf_loaded = [sem(n) for n in ("w_staged", "wo_loaded", "wf_loaded")]
        half_ready, set_up, w_split = sem("half_ready"), sem("set_up"), sem("w_split")
        first_staged, first_high, first_split = sem("first_staged"), sem("first_high"), sem("first_split")
        hin_ready, ta_ps, ta_free, xs_high_ready = [sem(n) for n in ("hin_ready", "ta_ps", "ta_free", "xs_high_ready")]
        qkv_ps, sq_ready, u_ready, w_ready, v_ready, rot_ready = [sem(n) for n in (
            "qkv_ps", "sq_ready", "u_ready", "w_ready", "v_ready", "rot_ready")]
        ss_ready = [sem("ss_ready0"), sem("ss_ready1")]
        ssm_ready, rn_ready, rq_ready, kn_ready = [sem(n) for n in ("ssm_ready", "rn_ready", "rq_ready", "kn_ready")]
        w_high_ready = sem("w_high_ready")
        s_ps, nb_ready = sem("s_ps"), sem("nb_ready")
        s_free = [sem("s_free0"), sem("s_free1")]
        exp_ready = [sem("exp_ready0"), sem("exp_ready1")]
        tp_ps, tp_free, ppT_ready = sem("tp_ps"), sem("tp_free"), sem("ppT_ready")
        o_ps, rden_ready, pn_ready, o_free = [sem(n) for n in ("o_ps", "rden_ready", "pn_ready", "o_free")]
        f_ps, f_free = sem("f_ps"), sem("f_free")
        hb_ready, hs_ready, fst_ready, fmv_ready, fve_ready, frstd_ready, xn_ready = [sem(n) for n in (
            "hb_ready", "hs_ready", "fst_ready", "fmv_ready", "fve_ready", "frstd_ready", "xn_ready")]
        block = ctx.enter_context(nc.Block())
        ident, down, carry = const["ident"], const["down"], const["carry"]

        V0, O0, F0, W0 = 2, len(O_USE) * TPS, len(F_USE) * NB, 4

        def ta(i, t, part, k):
            return len(TA_USE) * (TPS * i + t) + TA_USE[part, k]

        def tp(i, t, part, k):
            return len(TP_USE) * (TPS * i + t) + TP_USE[part, k]

        def ou(i, t, part, k):
            return len(O_USE) * (TPS * i + t) + O_USE[part, k]

        def fu(i, part, k):
            return len(F_USE) * i + F_USE[part, k]

        def heads8(ap):
            return ap.rearrange("p (h d) -> p h d", d=DH)

        def blocks4(ap):
            return ap.rearrange("p (a x) -> p a x", x=P)

        def first_stage(c):
            return qk[:, c, :] if c < 4 else sq[:, c - 4, :]

        @block.sync
        def _(sp):
            def stage(l, c):
                sp.dma_start(wstage[:, :], w["Wqkv"][l][:, bass.ds(c * WSTAGE, WSTAGE)]).then_inc(w_staged, 16)

            def load_wo(l):
                sp.dma_start(wo[:, :, :], w["Wo"][l].rearrange("(k p) c -> p k c", p=P)).then_inc(wo_loaded, 16)

            def load_ffn(l):
                sp.dma_start(w1[:, :], w["W1"][l]).then_inc(wf_loaded, 16)
                for c, (r0, n) in enumerate(FCH):
                    sp.dma_start(w2[0:n, c, :], w["W2"][l, r0:r0 + n, :]).then_inc(wf_loaded, 16)
                for a in range(2):
                    for c, (r0, n) in enumerate(FCH):
                        sp.dma_start(b1[0:n, a, c:c + 1],
                                     w["b1"][l, a * DI + r0:a * DI + r0 + n].unsqueeze(1)).then_inc(wf_loaded, 16)
                sp.dma_start(b2[:, :], w["b2"][l].partition_broadcast(P)).then_inc(wf_loaded, 16)
                sp.dma_start(ln_g[:, :], w["ln_g"][l].unsqueeze(1)).then_inc(wf_loaded, 16)
                sp.dma_start(ln_b[:, :], w["ln_b"][l].unsqueeze(1)).then_inc(wf_loaded, 16)

            for c in range(6):
                sp.dma_start(first_stage(c), w["Wqkv"][0][:, CH * c:CH * (c + 1)]).then_inc(first_staged, 16)
            load_wo(0)
            stage(1, 0)
            load_ffn(0)
            with sp.Fori(0, DEPTH - 1) as l:
                for c in range(1, NB):
                    sp.wait_ge(w_split, NB * (l + 1) + c)
                    stage(l + 1, c)
                sp.wait_ge(w_split, NB * (l + 2))
                stage((l + 2) % DEPTH, 0)
                sp.wait_ge(o_ps, len(O_USE) * TILES * (l + 1))
                load_wo(l + 1)
                sp.wait_ge(f_free, F0 + len(F_USE) * NB * (l + 1))
                load_ffn(l + 1)
            for c in range(1, NB):
                sp.wait_ge(w_split, NB * DEPTH + c)
                stage(0, c)

        N_WF = 16 * (1 + LF + 2 * LF + 3)

        @block.gpsimd
        def _(pool):
            nc.gpsimd.memset(minus_half[:], -0.5).then_inc(half_ready, 1)
            pool.wait_ge(half_ready, 1)
            pool.wait_ge(set_up, 1)

            layer_norm_pool(nc, pool, ln)

            def split(n, slot, c):
                cols = bass.ds(c * WSTAGE, WSTAGE)
                pool.wait_ge(w_staged, 16 * (n + 1))
                pool.nop(nofuse=True)
                nc.gpsimd.tensor_copy(w_high[:, slot, cols], wstage[:]).then_inc(w_high_ready, 1)
                pool.wait_ge(w_high_ready, n + 1)
                nc.gpsimd.tensor_tensor(w_low[:, slot, cols], wstage[:], w_high[:, slot, cols],
                                        ALU.subtract).then_inc(w_split, 1)

            def emit(i, l, x):
                part, t, k = x
                g = TPS * i + t
                if part == "in":
                    pool.wait_ge(f_free, len(F_USE) * (i + 1))
                    pool.wait_ge(o_free, len(O_USE) * (g + 1))
                    pool.nop(nofuse=True)
                    nc.gpsimd.tensor_copy(h_in[:, t, :], h[:, (i % NB) * TPS + t, :]).then_inc(hin_ready, 1)
                elif part == "split":
                    pool.wait_ge(qkv_ps, 6 * TPS * i + 1)
                    split(i, (l + 1) % 2, i % NB)
                elif part == "rotate":
                    pool.wait_ge(w_ready, 4 * g + k + 1)
                    nc.gpsimd.tensor_tensor(qk[:, k, :], qk[:, k, :], swap[:, k % 2, :],
                                            ALU.add).then_inc(rot_ready, 1)
                elif part == "weigh":
                    lo = 0 if t else WIN
                    pool.wait_ge(rden_ready, 4 * g + k + 1)
                    group = pr[:, 4 * k:4 * k + 4, lo:KEYS]
                    nc.gpsimd.tensor_tensor(group, group, rden[:, 4 * k:4 * k + 4].unsqueeze(2).broadcast_to(
                        [P, 4, KEYS - lo]), ALU.mult).then_inc(pn_ready, 1)
                elif part == "norm":
                    pool.wait_ge(ssm_ready, 2 * g + k + 1)
                    nc.gpsimd.tensor_tensor(rn[:, k, :], ssm[:, k, :], minus_half[:], ALU.pow).then_inc(rn_ready, 1)
                elif part == "shift":
                    pool.wait_ge(o_free, O0 + len(O_USE) * TPS * (i + 1))
                    pool.nop(nofuse=True)
                    nc.gpsimd.tensor_copy(hs[:, :, 0:C // 2], h_mid[:, :, 0:C // 2]).then_inc(hs_ready, 1)
                    pool.wait_ge(wf_loaded, N_WF * (l + 1))
                    nc.gpsimd.tensor_tensor(hb[:], h_mid[:], b2[:].unsqueeze(1).broadcast_to([P, TPS, C]),
                                            ALU.add).then_inc(hb_ready, 1)
                elif part == "stats":
                    pool.wait_ge(fve_ready, i + 1)
                    nc.gpsimd.tensor_tensor(frstd[:], fve[:], minus_half[:, 0:TPS], ALU.pow).then_inc(frstd_ready, 1)

            run_steps(pool, "POOL", emit)

        @block.scalar
        def _(act):
            act.wait_ge(set_up, 1)
            act.wait_ge(first_staged, 16 * 6)
            for c in range(6):
                nc.scalar.activation(w_high[:, 0, CH * c:CH * (c + 1)], first_stage(c),
                                     ACT.Copy).then_inc(first_high, 1)

            def emit(i, l, x):
                part, t, k = x
                g = TPS * i + t
                if part == "in":
                    act.wait_ge(ta_ps, ta(i, t, part, k) + 1)
                    nc.scalar.activation(xs_high[0:64, P * t:P * (t + 1)], TA[0:64, 0:P], ACT.Copy)
                    nc.scalar.activation(xs_high[64:128, P * t + 1:P * (t + 1) + 1], TA[64:128, 0:P],
                                         ACT.Copy).then_inc(xs_high_ready, 1)
                elif part == "qkv" and k < 4:
                    act.wait_ge(qkv_ps, 6 * g + k + 1)
                    act.wait_ge(ss_ready[k % 2], 1 + 2 * g + k // 2)
                    nc.scalar.activation(sq[:, k % 2, :], QKV[k % 2][:, :], ACT.Square).then_inc(sq_ready, 1)
                elif part == "qkv":
                    act.wait_ge(qkv_ps, 6 * g + k + 1)
                    nc.scalar.activation(v[:, t, 8 * (k - 4):8 * (k - 3), 0:DH], heads8(QKV[k % 2][:, :]),
                                         ACT.Copy).then_inc(v_ready, 1)
                elif part == "rot":
                    act.wait_ge(ta_ps, ta(i, t, part, k) + 1)
                    src = blocks4(TA[:, :])
                    if k < 2:
                        last = nc.scalar.activation(qT[:, t % 2, 4 * k:4 * k + 4, :], src, ACT.Copy)
                    else:
                        a = 4 * (k - 2)
                        last = nc.scalar.activation(kT[:, t, a:a + 4, WIN:KEYS], src, ACT.Copy)
                        if t < TPS - 1:
                            last = nc.scalar.activation(kT[:, t + 1, a:a + 4, 0:WIN], src[:, :, P - WIN:P], ACT.Copy)
                    last.then_inc(ta_free, 1)
                elif part == "s":
                    lo = 0 if t else WIN
                    act.wait_ge(nb_ready, PAIRS * g + k + 1)
                    for hd in unit_heads(k):
                        last = nc.scalar.activation(pr[:, hd, lo:KEYS], pr[:, hd, lo:KEYS], ACT.Exp,
                                                    bias=nb[:, hd:hd + 1], scale=nrq8[:, t, hd:hd + 1],
                                                    accum_out=row_sum[:, hd:hd + 1])
                    last.then_inc(exp_ready[k % 2], 1)
                elif part == "pt":
                    act.wait_ge(tp_ps, tp(i, t, part, k) + 1)
                    nc.scalar.activation(prT[:, k % 2, :, :], blocks4(TP[:, :]), ACT.Copy).then_inc(tp_free, 1)
                elif part == "pv":
                    act.wait_ge(o_ps, ou(i, t, part, k) + 1)
                    nc.scalar.activation(oT[:, 0:4, :], blocks4(O[:, :]), ACT.Copy).then_inc(o_free, 1)
                elif part == "xnT":
                    act.wait_ge(f_ps, fu(i, part, k) + 1)
                    act.wait_ge(wf_loaded, N_WF * (l + 1))
                    nc.scalar.activation(xnT[:], FB[:, :], ACT.Identity, bias=ln_b[:, 0:1],
                                         scale=ln_g[:, 0:1]).then_inc(f_free, 1)
                elif part == "gate":
                    n = FCH[k][1]
                    act.wait_ge(f_ps, fu(i, part, k) + 1)
                    nc.scalar.activation(gate[0:n, k, :], FB[0:n, :], ACT.Gelu,
                                         bias=b1[0:n, 1, k:k + 1]).then_inc(f_free, 1)

            run_steps(act, "ACT", emit)

        @block.vector
        def _(dve):
            for sm, n in ((o_free, O0), (w_split, NB), (v_ready, V0), (ppT_ready, W0), (ta_free, 1),
                          (tp_free, 1), (s_free[0], 1),
                          (s_free[1], 1), (ss_ready[0], 1), (ss_ready[1], 1), (hb_ready, 1)):
                dve.sem_inc(sm, n)
            nc.vector.tensor_copy(xs_high[:, 0:1], const["zero"])
            nc.vector.tensor_copy(xs_low[:, 0:1], const["zero"]).then_inc(set_up, 1)
            layer_norm_vector(nc, dve, ln, x, h)
            dve.wait_ge(ln["h_ready"], TILES)
            dve.sem_inc(f_free, F0)
            for c in range(6):
                cols = slice(CH * c, CH * (c + 1))
                dve.wait_ge(first_high, c + 1)
                nc.vector.tensor_tensor(w_low[:, 0, cols], first_stage(c), w_high[:, 0, cols],
                                        ALU.subtract).then_inc(first_split, 1)

            def emit(i, l, x):
                part, t, k = x
                g = TPS * i + t
                if part == "in":
                    dve.wait_ge(xs_high_ready, g + 1)
                    for r, col in ((slice(0, 64), P * t), (slice(64, 128), P * t + 1)):
                        last = nc.vector.tensor_tensor(xs_low[r, col:col + P], TA[r, 0:P], xs_high[r, col:col + P],
                                                       ALU.subtract)
                    last.then_inc(ta_free, 1)
                elif part == "rotate":
                    n = 4 * g + k
                    src = heads8(QKV[k % 2][:, :])
                    cos = tabs[:, l, t, 2 * (k // 2), :].unsqueeze(1).broadcast_to([P, 8, DH])
                    dve.wait_ge(sq_ready, n + 1)
                    nc.vector.tensor_tensor(heads8(qk[:, k, :]), src, cos, ALU.mult)
                    if k >= 2:
                        dve.wait_ge(rot_ready, n - 1)
                    for a, b in ((0, DH // 2), (DH // 2, 0)):
                        sn = tabs[:, l, t, 2 * (k // 2) + 1, a:a + DH // 2].unsqueeze(1).broadcast_to(
                            [P, 8, DH // 2])
                        last = nc.vector.tensor_tensor(heads8(swap[:, k % 2, :])[:, :, a:a + DH // 2],
                                                       src[:, :, b:b + DH // 2], sn, ALU.mult)
                    last.then_inc(w_ready, 1)
                    nc.vector.tensor_reduce(ss[:, k // 2, 8 * (k % 2):8 * (k % 2) + 8], heads8(sq[:, k % 2, :]), AX,
                                            ALU.add).then_inc(ss_ready[k % 2], 1)
                elif part == "norm":
                    for b in range(2):
                        dve.wait_ge(ss_ready[b], 1 + 2 * g + k + 1)
                    nc.vector.tensor_scalar(ssm[:, k, :], ss[:, k, :], 1e-24, None, ALU.max).then_inc(ssm_ready, 1)
                elif part == "scale":
                    dve.wait_ge(rn_ready, 2 * g + k + 1)
                    if k == 0:
                        nc.vector.tensor_scalar(rq8[:, t, :], rn[:, 0, :], QK_SCALE, None, ALU.mult)
                        nc.vector.tensor_scalar(nrq8[:, t, :], rn[:, 0, :], -QK_SCALE, None,
                                                ALU.mult).then_inc(rq_ready, 1)
                    else:
                        for c in range(2, 4):
                            dve.wait_ge(rot_ready, 4 * g + c + 1)
                            r = rn[:, 1, 8 * (c - 2):8 * (c - 1)].unsqueeze(2).broadcast_to([P, 8, DH])
                            nc.vector.tensor_tensor(heads8(qk[:, c, :]), heads8(qk[:, c, :]), r,
                                                    ALU.mult).then_inc(kn_ready, 1)
                elif part == "s":
                    lo = 0 if t else WIN
                    dve.wait_ge(s_ps, PAIRS * g + k + 1)
                    if k % 2 == 0 and t != 1:
                        dve.wait_ge(ppT_ready, W0 + 4 * (TPS - 1) * i + 4 * (t - 2 if t else -1) + k // 2 + 1)
                    dve.nop(nofuse=True)
                    for hh, hd in enumerate(unit_heads(k)):
                        last = nc.vector.tensor_tensor_reduce(
                            pr[:, hd, lo:KEYS], S[k % 2][:, hh * KEYS + lo:(hh + 1) * KEYS], const["mask"][:, lo:KEYS],
                            -1.0, HUGE, ALU.add, ALU.min, mn[:, hd:hd + 1])
                    last.then_inc(s_free[k % 2], 1)
                elif part == "nb":
                    if k == 0:
                        dve.wait_ge(rq_ready, g + 1)
                    dve.wait_ge(s_free[k % 2], 1 + PAIRS // 2 * g + k // 2 + 1)
                    hs2 = slice(unit_heads(k)[0], unit_heads(k)[1] + 1, 2)
                    nc.vector.tensor_tensor(nb[:, hs2], mn[:, hs2], rq8[:, t, hs2], ALU.mult).then_inc(nb_ready, 1)
                elif part == "pt" and t:
                    dve.wait_ge(pn_ready, 4 * g + k + 1)
                    nc.vector.transpose(ppT[96:128, 4 * k:4 * k + 4, :],
                                        pr[0:WIN, 4 * k:4 * k + 4, 0:WIN]).then_inc(ppT_ready, 1)
                elif part == "weigh":
                    for b in range(2):
                        dve.wait_ge(exp_ready[b], PAIRS // 2 * g + k + 1)
                    nc.vector.reciprocal(rden[:, 4 * k:4 * k + 4], row_sum[:, 4 * k:4 * k + 4]).then_inc(rden_ready, 1)
                elif part == "pv":
                    dve.wait_ge(o_ps, ou(i, t, part, k) + 1)
                    nc.vector.tensor_copy(oT[:, 4:8, :], blocks4(O[:, :])).then_inc(o_free, 1)
                elif part == "wo":
                    dve.wait_ge(o_ps, ou(i, t, part, k) + 1)
                    if t == 0:
                        dve.wait_ge(hb_ready, i + 1)
                    nc.vector.tensor_tensor(h_mid[:, t, :], h_in[:, t, :], O[:, 0:C], ALU.add).then_inc(o_free, 1)
                elif part == "shift":
                    dve.wait_ge(f_ps, fu(i, part, k) + 1)
                    nc.vector.tensor_copy(hs[:, :, C // 2:C], FB[:, 0:TPS * C // 2].rearrange(
                        "p (t x) -> p t x", x=C // 2)).then_inc(f_free, 1)
                elif part == "stats":
                    dve.wait_ge(f_free, F0 + fu(i, "shift", 0) + 1)
                    dve.wait_ge(hs_ready, i + 1)
                    for u in range(TPS):
                        nc.vector.bn_stats(fstats[:, u, :], hs[:, u, :]).then_inc(fst_ready, 1)
                    for u in range(TPS):
                        dve.wait_ge(fst_ready, TPS * i + u + 1)
                        dve.nop(nofuse=True)
                        nc.vector.bn_aggr(fmv[:, u, :], fstats[:, u, :]).then_inc(fmv_ready, 1)
                    dve.wait_ge(fmv_ready, TPS * i + TPS)
                    nc.vector.tensor_scalar(fve[:], fmv[:, :, 1], EPS, None, ALU.add).then_inc(fve_ready, 1)
                elif part == "ln":
                    dve.wait_ge(frstd_ready, i + 1)
                    for u in range(TPS):
                        nc.vector.tensor_scalar(hs[:, u, :], hs[:, u, :], fmv[:, u, 0:1], frstd[:, u:u + 1],
                                                ALU.subtract, ALU.mult).then_inc(xn_ready, 1)
                elif part == "lin":
                    n = FCH[k][1]
                    dve.wait_ge(f_ps, fu(i, part, k) + 1)
                    nc.vector.scalar_tensor_tensor(out=gate[0:n, k, :], in0=FB[0:n, :], scalar=b1[0:n, 0, k:k + 1],
                                                   in1=gate[0:n, k, :], op0=ALU.add, op1=ALU.mult
                                                   ).then_inc(f_free, 1)
                elif part == "out":
                    dve.wait_ge(f_ps, fu(i, part, k) + 1)
                    dve.wait_ge(hb_ready, 1 + i + 1)
                    nc.vector.tensor_tensor(h[:, bass.ds((i % NB) * TPS, TPS), :], hb[:],
                                            FB[:, :].rearrange("p (t c) -> p t c", c=C), ALU.add).then_inc(f_free, 1)

            run_steps(dve, "DVE", emit)

        @block.tensor
        def _(pe):
            pe.wait_ge(set_up, 1)
            pe.wait_ge(first_split, 6)

            def emit(i, l, x):
                part, t, k = x
                g = TPS * i + t
                if part == "in":
                    pe.wait_ge(hin_ready, g + 1)
                    pe.wait_ge(ta_free, 1 + ta(i, t, part, k))
                    nc.tensor.transpose(TA[:, 0:P], h_in[:, t, :], ident).then_inc(ta_ps, 1)
                elif part == "qkv":
                    if k == 0:
                        pe.wait_ge(ta_free, 1 + ta(i, t, "in", 0) + 1)
                        if t == 0:
                            pe.wait_ge(w_split, NB * (l + 1))
                    if k < 2:
                        pe.wait_ge(v_ready, V0 - 2 + 2 * g + k + 1)
                    else:
                        pe.wait_ge(w_ready, 4 * g + k - 1)
                    terms = ((xs_high, w_high), (xs_high, w_low), (xs_low, w_high))
                    for n, (a, b) in enumerate(terms):
                        last = nc.tensor.matmul(QKV[k % 2][:, :], a[:, P * t:P * (t + 1)],
                                                b[:, l % 2, CH * k:CH * (k + 1)], start=(n == 0), stop=(n == 2))
                    last.then_inc(qkv_ps, 1)
                elif part == "rot":
                    if k < 2:
                        pe.wait_ge(rot_ready, 4 * g + k + 1)
                    else:
                        pe.wait_ge(kn_ready, 2 * g + k - 1)
                    pe.wait_ge(ta_free, 1 + ta(i, t, part, k))
                    for a in range(4):
                        last = nc.tensor.transpose(TA[:, P * a:P * (a + 1)], qk[:, k, P * a:P * (a + 1)], ident)
                    last.then_inc(ta_ps, 1)
                elif part == "s":
                    lo = 0 if t else WIN
                    if k == 0:
                        pe.wait_ge(ta_free, 1 + ta(i, t, "rot", 3) + 1)
                    pe.wait_ge(s_free[k % 2], 1 + PAIRS // 2 * g + k // 2)
                    sv = S[k % 2][:, 0:2 * KEYS].rearrange("p (h x) -> p h x", x=KEYS)
                    r = slice(DH * (k % 2), DH * (k % 2) + DH)
                    for hh, hd in enumerate(unit_heads(k)):
                        last = nc.tensor.matmul(sv[:, hh, lo:KEYS], qT[r, t % 2, hd // 2, :],
                                                kT[r, t, hd // 2, lo:KEYS], start=True, stop=True)
                    last.then_inc(s_ps, 1)
                elif part == "pt":
                    pe.wait_ge(tp_free, 1 + tp(i, t, part, k))
                    pe.wait_ge(pn_ready, 4 * g + k + 1)
                    for a in range(4):
                        last = nc.tensor.transpose(TP[:, P * a:P * (a + 1)], pr[:, 4 * k + a, WIN:KEYS], ident)
                    last.then_inc(tp_ps, 1)
                elif part == "pv":
                    pe.wait_ge(tp_free, 1 + tp(i, t, "pt", k) + 1)
                    if k == 0:
                        pe.wait_ge(v_ready, V0 + 2 * g + 2)
                    if t:
                        pe.wait_ge(ppT_ready, W0 + 4 * (TPS - 1) * i + 4 * (t - 1) + k + 1)
                    if k % 2 == 0:
                        pe.wait_ge(o_free, O0 + ou(i, t, part, k + 1))
                    def place(hd, n):
                        col = 2 * P * (k % 2) + P * (hd // 2 - 2 * k)
                        return O[DH * (hd % 2):DH * (hd % 2) + DH, col:col + n]
                    for hd in range(4 * k, 4 * k + 4):
                        last = nc.tensor.matmul(place(hd, P), v[:, t, hd, :], prT[:, k % 2, hd - 4 * k, :],
                                                start=True, stop=not t, skip_group_check=True)
                        if t:
                            last = nc.tensor.matmul(place(hd, WIN), v[96:128, t - 1, hd, :], ppT[96:128, hd, :],
                                                    start=False, stop=True, skip_group_check=True)
                    if k % 2:
                        last.then_inc(o_ps, 1)
                elif part == "wo":
                    if t == 0:
                        pe.wait_ge(wo_loaded, 16 * (l + 1))
                    pe.wait_ge(o_free, O0 + ou(i, t, part, k))
                    for c in range(PAIRS):
                        last = nc.tensor.matmul(O[:, 0:C], oT[:, c, :], wo[:, c, :], start=(c == 0),
                                                stop=(c == PAIRS - 1))
                    last.then_inc(o_ps, 1)
                elif part == "shift":
                    pe.wait_ge(o_free, O0 + len(O_USE) * TPS * (i + 1))
                    pe.wait_ge(f_free, F0 + fu(i, part, k))
                    nc.tensor.matmul(FB[:, 0:TPS * 64], down, h_mid[:, :, 64:128], start=True, stop=False,
                                     skip_group_check=True)
                    nc.tensor.matmul(FB[:, 64:TPS * 64], carry, h_mid[:, 0:TPS - 1, 64:128], start=False,
                                     stop=True, skip_group_check=True).then_inc(f_ps, 1)
                elif part == "xnT":
                    pe.wait_ge(xn_ready, TPS * i + TPS)
                    pe.wait_ge(f_free, F0 + fu(i, part, k))
                    for u in range(TPS):
                        last = nc.tensor.transpose(FB[:, P * u:P * (u + 1)], hs[:, u, :], ident)
                    last.then_inc(f_ps, 1)
                elif part in ("gate", "lin"):
                    a = int(part == "gate")
                    r0, n = FCH[k]
                    if a and k == 0:
                        pe.wait_ge(wf_loaded, N_WF * (l + 1))
                    pe.wait_ge(f_free, F0 + fu(i, part, k))
                    nc.tensor.matmul(FB[0:n, :], w1[:, a * DI + r0:a * DI + r0 + n], xnT[:], start=True,
                                     stop=True).then_inc(f_ps, 1)
                elif part == "out":
                    pe.wait_ge(f_free, F0 + fu(i, part, k))
                    for u in range(TPS):
                        for c, (_, n) in enumerate(FCH):
                            last = nc.tensor.matmul(FB[:, C * u:C * (u + 1)], gate[0:n, c, P * u:P * (u + 1)],
                                                    w2[0:n, c, :], start=(c == 0), stop=(c == LF - 1))
                    last.then_inc(f_ps, 1)

            run_steps(pe, "PE", emit)


def alibi_phase(nc, x, h, const, w):
    units = TPS * H2
    GR = H2 // 4
    TABW = 2 * NT - P
    slopes = alibi_slopes()
    LAG_T, LAG_PV, LAG_OT, LAG_OB, LAG_ON, LAG_WP = 3, 5, 5, 7, 8, 10
    FRONT = {"z": units - 4, **{c: units + c for c in range(2 * GR)}, "v": units + 2 * GR}
    stage_at = {at: n for n, at in FRONT.items()}
    SL = 4

    with ExitStack() as ctx:
        def sb(n, shape, dt=F32):
            return ctx.enter_context(nc.sbuf_tensor(f"al_{n}", shape, dt))

        def ps(n):
            return ctx.enter_context(nc.psum_tensor(f"al_{n}", [P, 512], F32))

        sem = ctx.enter_context(phase_semaphores(nc, "al"))
        ln = layer_norm_parts(sb, sem, sb("ln_stats", [P, TILES, 6]))

        wraw = sb("wraw", [P, 3 * C])
        wpad = sb("wpad", [P, 2, GR, 4, 4, D2])
        brow = sb("brow", [1, 2 * C])
        bwide = sb("bwide", [1, 2, GR, 4, 4, D2])
        one = sb("one", [1, 1])
        bpad = sb("bpad", [P, 2, GR])
        low = sb("low", [P, 2])
        bqs = sb("bqs", [P, GR])
        bv, bo = sb("bv", [P, C]), sb("bo", [P, C])
        wp = sb("wp", [P, C])
        dist = sb("dist", [P, TABW])
        tab = sb("tab", [P, H2, TABW])
        z = sb("z", [P, TPS, C])
        zT = sb("zT", [P, NT])
        full = sb("full", [P, 2, NT])
        high = sb("high", [P, 2, NT], F32R)
        qkT = sb("qkT", [P, 2 * GR, NT], F32R)
        v = sb("v", [P, TPS, H2, 32])
        sc = sb("sc", [P, SL, NT])
        nm = sb("nm", [P, units])
        pr = sb("pr", [P, SL, NT])
        prT = sb("prT", [P, SL, NT])
        rden = sb("rden", [P, H2])
        on = sb("on", [P, H2, D2])
        oT = sb("oT", [P, NT])
        onT = sb("onT", [P, P])
        S = [ps("psS0"), ps("psS1")]
        T = [ps("psT0"), ps("psT1")]
        A = [ps("psA0"), ps("psA1")]
        M, N = ps("psM"), ps("psN")

        (loaded, zeroed, pad_ready, tab_ready, xb_ready, z_ready, zT_ps, zT_ready, v_ps, v_ready,
         s_ps, sc_ready, exp_ready, pT_ps, pv_ps, rden_ready, on_ready, onT_ps, onT_ready, y_ps, x_done,
         high_ready, oT_ready, oN_ps, bt_ps) = [sem(n) for n in (
             "loaded", "zeroed", "pad_ready", "tab_ready", "xb_ready", "z_ready", "zT_ps",
             "zT_ready", "v_ps", "v_ready", "s_ps", "sc_ready", "exp_ready", "pT_ps", "pv_ps", "rden_ready",
             "on_ready", "onT_ps", "onT_ready", "y_ps", "x_done", "high_ready", "oT_ready", "oN_ps", "bt_ps")]
        qk_ps = sem("qk_ps")
        qk_ready, x_mixed = sem("qk_ready"), sem("x_mixed")
        pT_ready = [sem("pT_ready0"), sem("pT_ready1")]
        block = ctx.enter_context(nc.Block())
        ident = const["ident"]
        N_LOAD = 16 * 7

        @block.sync
        def _(sp):
            sp.dma_start(wraw[:], w["W_qkv"][:, :]).then_inc(loaded, 16)
            sp.dma_start(wp[:], w["W_proj"][:, :]).then_inc(loaded, 16)
            sp.dma_start(bv[:], w["b_qkv"][2 * C:3 * C].partition_broadcast(P)).then_inc(loaded, 16)
            sp.dma_start(bo[:], w["b_proj"][:].partition_broadcast(P)).then_inc(loaded, 16)
            sp.dma_start(dist[:], w["dist"][:, :]).then_inc(loaded, 16)
            sp.dma_start(brow[:], w["b_qkv"][0:2 * C].unsqueeze(0)).then_inc(loaded, 16)
            sp.dma_start(low[:], w["low"]).then_inc(loaded, 16)

        @block.gpsimd
        def _(pool):
            layer_norm_pool(nc, pool, ln)
            pool.wait_ge(ln["h_ready"], TILES)
            pool.wait_ge(loaded, N_LOAD)
            nc.gpsimd.tensor_tensor(x[:], x[:], bo[:].unsqueeze(1).broadcast_to([P, TILES, C]),
                                    ALU.add).then_inc(xb_ready, 1)
            nc.gpsimd.tensor_copy(z[:], h[:, 0:TPS, :]).then_inc(z_ready, 1)
            with pool.Fori(0, NB) as b:
                pool.wait_ge(zT_ps, CREDIT + b + 1)
                nc.gpsimd.tensor_copy(z[:], h[:, bass.ds((b + 1) % NB * TPS, TPS), :]).then_inc(z_ready, 1)

        @block.scalar
        def _(act):
            act.wait_ge(pad_ready, 2)

            def front(f, n):
                if n == "z":
                    act.wait_ge(zT_ps, CREDIT + f + 1)
                    nc.scalar.activation(zT[:], N[:, :], ACT.Copy).then_inc(zT_ready, 1)
                elif n in range(2 * GR):
                    act.wait_ge(qk_ps, 2 * GR * f + n + 1)
                    act.wait_ge(qk_ready, 2 * CREDIT + 2 * GR * f + n - 1)
                    bias = bqs[:, n:n + 1] if n < GR else bpad[:, 1, n - GR:n - GR + 1]
                    scale = float(D2) ** -0.5 if n < GR else 1.0
                    nc.scalar.activation(full[:, n % 2, :], S[n % 2][:, :], ACT.Identity, bias=bias, scale=scale)
                    nc.scalar.activation(high[:, n % 2, :], S[n % 2][:, :], ACT.Identity, bias=bias,
                                         scale=scale).then_inc(high_ready, 1)

            for n in FRONT:
                front(0, n)
            with act.Fori(0, NB) as b:
                for k in range(units + LAG_WP + 2):
                    if k < units:
                        act.wait_ge(sc_ready, CREDIT + units * b + k + 1)
                        if k >= SL:
                            act.wait_ge(pT_ps, units * b + k - SL + 1)
                        nc.scalar.activation(pr[:, k % SL, :], sc[:, k % SL, :], ACT.Exp, bias=nm[:, k:k + 1],
                                             scale=-1.0).then_inc(exp_ready, 1)
                    u = k - LAG_T
                    if 0 <= u < units and u % 2 == 0:
                        act.wait_ge(pT_ps, units * b + u + 1)
                        nc.scalar.activation(prT[:, u % SL, :], T[0][:, :], ACT.Copy).then_inc(pT_ready[0], 1)
                    if k >= H2 + LAG_OT and (k - LAG_OT) % H2 == 0:
                        qt = (k - LAG_OT) // H2 - 1
                        act.wait_ge(pv_ps, units * b + H2 * qt + H2)
                        nc.scalar.activation(oT[:], A[qt % 2][:, :], ACT.Copy).then_inc(oT_ready, 1)
                    if k >= H2 + LAG_ON + 1 and (k - LAG_ON - 1) % H2 == 0:
                        qt = (k - LAG_ON - 1) // H2 - 1
                        act.wait_ge(onT_ps, TPS * b + qt + 1)
                        nc.scalar.activation(onT[:], M[:, 0:P], ACT.Copy).then_inc(onT_ready, 1)
                    if k in stage_at:
                        front(b + 1, stage_at[k])

        @block.vector
        def _(dve):
            for sm in (zT_ps, exp_ready, onT_ready, on_ready, x_done, sc_ready, high_ready, oT_ready, *pT_ready):
                dve.sem_inc(sm, CREDIT)
            dve.sem_inc(qk_ready, 2 * CREDIT)
            for b in range(NB):
                sl = slice(b * TPS, (b + 1) * TPS)
                nc.vector.scalar_tensor_tensor(out=x[:, sl, :], in0=h[:, sl, :], scalar=0.5, in1=x[:, sl, :],
                                               op0=ALU.mult, op1=ALU.add).then_inc(x_mixed, 1)
            dve.wait_ge(x_mixed, NB)
            layer_norm_vector(nc, dve, ln, x, h)
            nc.vector.memset(one[:], 1.0)
            nc.vector.memset(v[:, :, :, D2 + 1:], 0.0)
            nc.vector.memset(v[:, :, :, D2:D2 + 1], 1.0).then_inc(zeroed, 1)
            dve.wait_ge(loaded, N_LOAD)
            for r in range(4):
                for dst, src in ((wpad, wraw), (bwide, brow)):
                    for n in range(2):
                        last = nc.vector.tensor_copy(dst[:, n, :, :, r, :], src[:, n * C:(n + 1) * C].rearrange(
                            "p (c j d) -> p c j d", j=4, d=D2))
            last.then_inc(pad_ready, 1)
            dve.wait_ge(bt_ps, 1)
            nc.vector.tensor_copy(bpad[:], M[:, 0:2 * GR].rearrange("p (n c) -> p n c", n=2))
            nc.vector.tensor_scalar(bqs[:], M[:, 0:GR], float(D2) ** -0.5, None, ALU.mult).then_inc(pad_ready, 1)
            for hd in range(H2):
                nc.vector.tensor_scalar(tab[:, hd, :], dist[:], slopes[hd], None, ALU.mult).then_inc(tab_ready, 1)
            dve.wait_ge(tab_ready, H2)

            def front(f, n):
                if n in range(2 * GR):
                    dve.wait_ge(high_ready, CREDIT + 2 * GR * f + n + 1)
                    nc.vector.scalar_tensor_tensor(out=qkT[:, n, :], in0=high[:, n % 2, :],
                                                   scalar=low[:, n // GR:n // GR + 1], in1=full[:, n % 2, :],
                                                   op0=ALU.mult, op1=ALU.add).then_inc(qk_ready, 1)
                elif n == "v":
                    dve.wait_ge(v_ps, f + 1)
                    nc.vector.tensor_tensor(v[:, :, :, 0:D2], T[0][:, :].rearrange("p (t h d) -> p t h d", h=H2, d=D2),
                                            bv[:].rearrange("p (h d) -> p h d", d=D2).unsqueeze(1).broadcast_to(
                                                [P, TPS, H2, D2]), ALU.add).then_inc(v_ready, 1)

            for n in FRONT:
                front(0, n)
            with dve.Fori(0, NB) as b:
                for k in range(units + LAG_WP + 2):
                    if k < units:
                        qt, hd = k // H2, k % H2
                        dve.wait_ge(s_ps, units * b + k + 1)
                        dve.wait_ge(exp_ready, CREDIT + units * b + max(k - SL + 1, 0))
                        off = NT - P - P * qt
                        dve.nop(nofuse=True)
                        nc.vector.tensor_tensor_reduce(sc[:, k % SL, :], S[k % 2][:, :], tab[:, hd, off:off + NT],
                                                       -1.0, HUGE, ALU.add, ALU.min, nm[:, k:k + 1]
                                                       ).then_inc(sc_ready, 1)
                    u = k - LAG_T
                    if 0 <= u < units and u % 2:
                        dve.wait_ge(pT_ps, units * b + u + 1)
                        nc.vector.tensor_copy(prT[:, u % SL, :], T[1][:, :]).then_inc(pT_ready[1], 1)
                    if k >= H2 + LAG_OB and (k - LAG_OB) % H2 == 0:
                        qt = (k - LAG_OB) // H2 - 1
                        ov = M[:, :].rearrange("p (h x) -> p h x", x=32)
                        dve.wait_ge(oN_ps, TPS * b + qt + 1)
                        nc.vector.reciprocal(rden[:], ov[:, :, D2]).then_inc(rden_ready, 1)
                        dve.wait_ge(rden_ready, TPS * b + qt + 1)
                        nc.vector.tensor_tensor(on[:], ov[:, :, 0:D2], rden[:].unsqueeze(2).broadcast_to([P, H2, D2]),
                                                ALU.mult).then_inc(on_ready, 1)
                    if k >= H2 + LAG_WP + 1 and (k - LAG_WP - 1) % H2 == 0:
                        qt = (k - LAG_WP - 1) // H2 - 1
                        dve.wait_ge(y_ps, TPS * b + qt + 1)
                        dve.wait_ge(xb_ready, 1)
                        nc.vector.tensor_tensor(x[:, b * TPS + qt, :], x[:, b * TPS + qt, :], N[:, 0:C],
                                                ALU.add).then_inc(x_done, 1)
                    if k in stage_at:
                        front(b + 1, stage_at[k])

        @block.tensor
        def _(pe):
            pe.wait_ge(pad_ready, 1)
            pe.wait_ge(zeroed, 1)
            pe.wait_ge(loaded, N_LOAD)
            for n in range(2):
                for c in range(GR):
                    last = nc.tensor.matmul(M[:, n * GR + c:n * GR + c + 1],
                                            bwide[:, n, c, :, :, :].rearrange("p j r d -> p (j r d)"), one[:],
                                            start=True, stop=True)
            last.then_inc(bt_ps, 1)
            pe.wait_ge(pad_ready, 2)

            def front(f, n, first):
                if n == "z":
                    pe.wait_ge(z_ready, f + 1)
                    if not first:
                        pe.wait_ge(x_done, CREDIT + TPS * f - 1)
                    for t in range(TPS):
                        last = nc.tensor.transpose(N[:, P * t:P * (t + 1)], z[:, t, :], ident)
                    last.then_inc(zT_ps, 1)
                elif n == "v":
                    for t in range(TPS):
                        last = nc.tensor.matmul(T[0][:, C * t:C * (t + 1)], zT[:, P * t:P * (t + 1)],
                                                wraw[:, 2 * C:3 * C], start=True, stop=True)
                    last.then_inc(v_ps, 1)
                else:
                    if n == 0:
                        pe.wait_ge(zT_ready, f + 1)
                    if n >= 2:
                        pe.wait_ge(high_ready, CREDIT + 2 * GR * f + n - 1)
                    elif not first:
                        pe.wait_ge(sc_ready, CREDIT + units * f - 1 + n)
                    nc.tensor.matmul(S[n % 2][:, :],
                                     wpad[:, n // GR, n % GR, :, :, :].rearrange("p j r d -> p (j r d)"),
                                     zT[:], start=True, stop=True).then_inc(qk_ps, 1)

            for n in FRONT:
                front(0, n, True)
            with pe.Fori(0, NB) as b:
                pe.wait_ge(qk_ready, 2 * CREDIT + 2 * GR * b + 2 * GR)
                pe.wait_ge(v_ready, b + 1)
                for k in range(units + LAG_WP + 2):
                    if k < units:
                        qt, hd = k // H2, k % H2
                        c, j = hd // 4, 32 * (hd % 4)
                        if k >= 2:
                            pe.wait_ge(sc_ready, CREDIT + units * b + k - 1)
                        nc.tensor.matmul(S[k % 2][:, :], qkT[j:j + 32, c, P * qt:P * (qt + 1)],
                                         qkT[j:j + 32, GR + c, :], start=True, stop=True).then_inc(s_ps, 1)
                    u = k - LAG_T
                    if 0 <= u < units:
                        pe.wait_ge(exp_ready, CREDIT + units * b + u + 1)
                        pe.wait_ge(pT_ready[u % 2], CREDIT + units // 2 * b + u // 2)
                        for a in range(TPS):
                            last = nc.tensor.transpose(T[u % 2][:, P * a:P * (a + 1)],
                                                       pr[:, u % SL, P * a:P * (a + 1)], ident)
                        last.then_inc(pT_ps, 1)
                    u = k - LAG_PV
                    if 0 <= u < units:
                        qt, hd = u // H2, u % H2
                        c, j = hd // 4, 32 * (hd % 4)
                        pe.wait_ge(pT_ready[u % 2], CREDIT + units // 2 * b + u // 2 + 1)
                        if hd == 0:
                            pe.wait_ge(oT_ready, CREDIT + TPS * b + max(qt - 1, 0))
                        for a in range(TPS):
                            last = nc.tensor.matmul(A[qt % 2][j:j + 32, P * c:P * (c + 1)], v[:, a, hd, :],
                                                    prT[:, u % SL, P * a:P * (a + 1)],
                                                    start=(a == 0), stop=(a == TPS - 1), skip_group_check=True)
                        last.then_inc(pv_ps, 1)
                    if k >= H2 + LAG_OB and (k - LAG_OB) % H2 == 0:
                        qt = (k - LAG_OB) // H2 - 1
                        pe.wait_ge(oT_ready, CREDIT + TPS * b + qt + 1)
                        pe.wait_ge(onT_ready, CREDIT + TPS * b + qt)
                        for c in range(GR):
                            last = nc.tensor.transpose(M[:, P * c:P * (c + 1)], oT[:, P * c:P * (c + 1)], ident)
                        last.then_inc(oN_ps, 1)
                    if k >= H2 + LAG_ON and (k - LAG_ON) % H2 == 0:
                        qt = (k - LAG_ON) // H2 - 1
                        pe.wait_ge(on_ready, CREDIT + TPS * b + qt + 1)
                        pe.wait_ge(onT_ready, CREDIT + TPS * b + qt)
                        nc.tensor.transpose(M[:, 0:P], on[:].rearrange("p h d -> p (h d)"), ident).then_inc(onT_ps, 1)
                    if k >= H2 + LAG_WP and (k - LAG_WP) % H2 == 0:
                        qt = (k - LAG_WP) // H2 - 1
                        pe.wait_ge(onT_ready, CREDIT + TPS * b + qt + 1)
                        pe.wait_ge(x_done, CREDIT + TPS * b + qt)
                        nc.tensor.matmul(N[:, 0:C], onT[:], wp[:], start=True, stop=True).then_inc(y_ps, 1)
                    if k in stage_at:
                        front(b + 1, stage_at[k], False)


def start_phase(nc, x, x_in, tabs, eye3, zero, mask, c_eye, c_mask, c_rot, q_scale, k_scale):
    with ExitStack() as ctx:
        rotary = ctx.enter_context(nc.sbuf_tensor("rotary", [P, TPS, 4, DH], F32))
        gain = ctx.enter_context(nc.sbuf_tensor("gain", [P, 2, DEPTH, DH], F32))
        sem = ctx.enter_context(phase_semaphores(nc, "c"))
        loaded, made, x_loaded = sem("loaded"), sem("made"), sem("x_loaded")
        block = ctx.enter_context(nc.Block())

        @block.sync
        def _(sp):
            sp.dma_start(rotary[:], c_rot).then_inc(loaded, 16)
            for n, g in enumerate((q_scale, k_scale)):
                sp.dma_start(gain[:, n, :, :].rearrange("p l d -> p (l d)"),
                             g.rearrange("l d -> (l d)").partition_broadcast(P)).then_inc(loaded, 16)
            sp.dma_start(eye3[:], c_eye).then_inc(loaded, 16)
            sp.dma_start(mask[:], c_mask).then_inc(loaded, 16)
            for b in range(NB):
                sp.dma_start(x[:, b * TPS:(b + 1) * TPS, :],
                             x_in[b].rearrange("(t p) c -> p t c", p=P)).then_inc(x_loaded, 16)
            sp.wait_ge(x_loaded, 16 * NB)

        def tables(eng, layers):
            half = DH // 2
            for l in layers:
                for n in range(2):
                    for a, b, m in ((0, DH, 0), (0, half, 1), (half, DH, 1)):
                        src = (a + half) % DH if m else a
                        g = gain[:, n, l, src:src + b - a].unsqueeze(1).broadcast_to([P, TPS, b - a])
                        last = eng.tensor_tensor(tabs[:, l, :, 2 * n + m, a:b], rotary[:, :, 2 * n + m, a:b], g,
                                                 ALU.mult)
            return last

        @block.gpsimd
        def _(pool):
            pool.wait_ge(loaded, 80)
            tables(nc.gpsimd, range(4, DEPTH)).then_inc(made, 1)

        @block.vector
        def _(dve):
            dve.wait_ge(loaded, 80)
            nc.vector.memset(zero[:], 0.0)
            tables(nc.vector, range(4)).then_inc(made, 1)


def build(nc, ins, out):
    with ExitStack() as ctx:
        def sb(n, shape, dt=F32):
            return ctx.enter_context(nc.sbuf_tensor(n, shape, dt))

        def constant(name, array, dt=F32):
            return nc.inline_tensor(np.ascontiguousarray(array), name).ap()

        eye3 = sb("eye3", [P, 3 * P])
        zero = sb("zero", [P, 1])
        mask = sb("mask", [P, KEYS])
        tabs = sb("tabs", [P, DEPTH, TPS, 4, DH])
        x = sb("x", [P, TILES, C])
        h = sb("h", [P, TILES, C])
        c_eye = constant("c_eye3", shift_matrices())
        c_mask = constant("c_mask", window_mask().astype(np.float32))
        c_rot = constant("c_rotary", rotary_constants())
        d = np.arange(2 * NT - P)[None, :] - (NT - P) - np.arange(P)[:, None]
        c_dist = constant("c_dist", np.minimum(d, 0).astype(np.float32))
        const = {"ident": eye3[:, 0:P], "down": eye3[:, P:2 * P], "carry": eye3[:, 2 * P:3 * P],
                 "zero": zero[:], "mask": mask[:], "tabs": tabs[:]}
        start_phase(nc, x, ins["L0_attn_x"], tabs, eye3, zero, mask, c_eye, c_mask, c_rot, ins["L0_ffn_q_scale"],
                      ins["L0_ffn_k_scale"])
        f_w = {n: ins["L0_ffn_" + n] for n in ("Wqkv", "q_scale", "k_scale", "Wo", "ln_g", "ln_b", "W1", "b1",
                                               "W2", "b2")}
        a_w = {n: ins["L0_attn_" + n] for n in ("W_qkv", "b_qkv", "W_proj", "b_proj")}
        a_w["dist"] = c_dist
        row = np.arange(P) % 32 // D2
        a_w["low"] = constant("c_low", -np.stack([row >= 2, row % 2 == 1], 1).astype(np.float32))
        macaron_phase(nc, "f1", x, h, const, f_w)
        alibi_phase(nc, x, h, const, a_w)
        macaron_phase(nc, "f2", x, h, const, f_w)
        output_phase(nc, x, h, out)


_INS = ["L0_attn_x", "L0_attn_W_qkv", "L0_attn_b_qkv", "L0_attn_W_proj", "L0_attn_b_proj", "L0_ffn_Wqkv",
        "L0_ffn_q_scale", "L0_ffn_k_scale", "L0_ffn_Wo", "L0_ffn_ln_g", "L0_ffn_ln_b", "L0_ffn_W1", "L0_ffn_b1",
        "L0_ffn_W2", "L0_ffn_b2"]


def kernel(**inputs):
    import concourse.bacc as bacc
    from concourse.bass_utils import run_bass_kernel_spmd

    nc = bacc.Bacc("TRN2", target_bir_lowering=False, num_devices=1)
    arrays, ins = {}, {}
    for name in _INS:
        a = np.ascontiguousarray(inputs[name])
        arrays[f"in_{name}"] = a
        ins[name] = nc.dram_tensor(f"in_{name}", a.shape, mybir.dt.from_np(a.dtype), kind="ExternalInput").ap()
    out = nc.dram_tensor("out_x", (NB, NT, C), F32, kind="ExternalOutput").ap()
    build(nc, ins, out)
    r = run_bass_kernel_spmd(nc, [arrays], core_ids=[0])
    return r.results[0]["out_x"]
```
